# Optimizing a Trainium2 kernel written in Bass

```python
import numpy as np
import jax
import jax.numpy as jnp

def _softmax(x, axis=-1):
    return jax.nn.softmax(x, axis=axis)

def _gelu(x):
    return jax.nn.gelu(x, approximate=True)

def _silu(x):
    return jax.nn.silu(x)

def _sigmoid(x):
    return jax.nn.sigmoid(x)

def _layernorm(x, axis=-1, eps=1e-05):
    m = jnp.mean(x, axis=axis, keepdims=True)
    v = jnp.var(x, axis=axis, keepdims=True)
    return (x - m) / jnp.sqrt(v + eps)

def _scatter_add(tgt, idx, src, axis=0):
    return tgt.at[idx].add(src)

def _segment_sum(src, seg, n):
    return jax.ops.segment_sum(src, seg, n)
kernel_name = 'mk_gnn_resnorm_d4_gnn_r8_777f32'

def setup_inputs(seed: int=0):
    np.random.seed(seed)
    _w = jnp.asarray

    def _rec_inputs():
        import jax
        import jax.numpy as jnp
        _gk = jax.random.key(seed)
        x = -0.000202 + 1 * jax.random.normal(jax.random.fold_in(_gk, 1), (6250, 128), jnp.float32)
        _s = jax.random.randint(jax.random.fold_in(_gk, 2), (50000,), 0, 6250, jnp.int32)
        _d = jax.random.randint(jax.random.fold_in(_gk, 3), (50000,), 0, 6250, jnp.int32)
        _loop = jnp.arange(6250, dtype=jnp.int32)
        src = jnp.concatenate([_s, _d, _loop])
        dst = jnp.concatenate([_d, _s, _loop])
        _o = jnp.argsort(dst, stable=True)
        src = src[_o]
        dst = dst[_o]
        edge_attr_128 = -5.16925e-05 + 1.00005 * jax.random.normal(jax.random.fold_in(_gk, 12), (106250, 128), jnp.float32)
        node_vec = -0.00396605 + 0.997609 * jax.random.normal(jax.random.fold_in(_gk, 14), (6250,), jnp.float32)
        return (x, src, dst, edge_attr_128, node_vec)
    x, src, dst, edge_attr_128, node_vec = _rec_inputs()

    def _L0_gnn_setup():
        import jax, jax.numpy as jnp
        import numpy as np
        N_NODES = 6250
        N_EDGES = 100000
        IN_CH = 128
        OUT_CH = 128
        key = jax.random.key(seed)
        k1, k2, k3, k4 = jax.random.split(key, 4)
        x = jax.random.normal(k1, (N_NODES, IN_CH), dtype=jnp.float32)
        edge_index = jax.random.randint(k2, (2, N_EDGES), 0, N_NODES, dtype=jnp.int64)
        W = jax.random.normal(k3, (OUT_CH, IN_CH), dtype=jnp.float32) / np.sqrt(IN_CH)
        b = jax.random.normal(k4, (OUT_CH,), dtype=jnp.float32) * 0.01
        agg_weight = jnp.ones((1,), dtype=jnp.float32)
        return {'x': x, 'edge_index': edge_index, 'W': W, 'b': b, 'agg_weight': agg_weight}
    _L0_gnn_all = _L0_gnn_setup()
    _L0_gnn_in = {k: v for k, v in _L0_gnn_all.items() if k in ('W', 'b', 'agg_weight')}
    del _L0_gnn_all

    def _L1_gnn_setup():
        import jax, jax.numpy as jnp
        import numpy as np
        N = 12500
        E = 200000
        D = 128
        NEG_SLOPE = 0.2

        def _edge_softmax(logits, dst, n):
            m = jax.ops.segment_max(logits, dst, num_segments=n)
            ex = jnp.exp(logits - m[dst])
            denom = jax.ops.segment_sum(ex, dst, num_segments=n)
            return ex / denom[dst]
        key = jax.random.key(seed)
        ks = jax.random.split(key, 8)
        s = 1.0 / np.sqrt(D)
        return {'feat': jax.random.normal(ks[0], (N, D), dtype=jnp.float32), 'simi_weight': jax.random.normal(ks[1], (N,), dtype=jnp.float32), 'W_homo': jax.random.normal(ks[2], (D, D), dtype=jnp.float32) * s, 'b_homo': jnp.zeros((D,), dtype=jnp.float32), 'W_hete': jax.random.normal(ks[3], (D, D), dtype=jnp.float32) * s, 'b_hete': jnp.zeros((D,), dtype=jnp.float32), 'W_self': jax.random.normal(ks[4], (D, D), dtype=jnp.float32) * s, 'b_self': jnp.zeros((D,), dtype=jnp.float32), 'src_idx': jax.random.randint(ks[5], (E,), 0, N, dtype=jnp.int32), 'dst_idx': jax.random.randint(ks[6], (E,), 0, N, dtype=jnp.int32)}
    _L1_gnn_all = _L1_gnn_setup()
    _L1_gnn_in = {k: v for k, v in _L1_gnn_all.items() if k in ('W_homo', 'b_homo', 'W_hete', 'b_hete', 'W_self', 'b_self')}
    del _L1_gnn_all

    def _L2_gnn_setup():
        import jax, jax.numpy as jnp
        import numpy as np
        N = 12500
        E = 125000
        D = 128
        OUT = 128
        key = jax.random.key(seed)
        k1, k2, k3, k4, k5 = jax.random.split(key, 5)
        feats = jax.random.normal(k1, (N, D), dtype=jnp.float32)
        src = jax.random.randint(k2, (E,), 0, N, dtype=jnp.int32)
        dst = jax.random.randint(k3, (E,), 0, N, dtype=jnp.int32)
        W = jax.random.normal(k4, (OUT, 3 * D), dtype=jnp.float32) * np.float32(1.0 / np.sqrt(3 * D))
        b = jax.random.normal(k5, (OUT,), dtype=jnp.float32) * np.float32(0.01)
        return {'feats': feats, 'W': W, 'b': b, 'src': src, 'dst': dst}
    _L2_gnn_all = _L2_gnn_setup()
    _L2_gnn_in = {k: v for k, v in _L2_gnn_all.items() if k in ('W', 'b')}
    del _L2_gnn_all

    def _L3_gnn_setup():
        import jax, jax.numpy as jnp
        import numpy as np
        N_NODES = 6250
        N_EDGES = 100000
        C = 128
        D = 128
        Z = 2 * C + D
        key = jax.random.key(seed)
        ks = jax.random.split(key, 7)
        x = jax.random.normal(ks[0], (N_NODES, C), dtype=jnp.float32)
        edge_index = jax.random.randint(ks[1], (2, N_EDGES), 0, N_NODES, dtype=jnp.int64)
        edge_attr = jax.random.normal(ks[2], (N_EDGES, D), dtype=jnp.float32)
        s = 1.0 / np.sqrt(Z)
        W_f = jax.random.uniform(ks[3], (Z, C), dtype=jnp.float32, minval=-s, maxval=s)
        b_f = jax.random.uniform(ks[4], (C,), dtype=jnp.float32, minval=-s, maxval=s)
        W_s = jax.random.uniform(ks[5], (Z, C), dtype=jnp.float32, minval=-s, maxval=s)
        b_s = jax.random.uniform(ks[6], (C,), dtype=jnp.float32, minval=-s, maxval=s)
        return {'x': x, 'edge_index': edge_index, 'edge_attr': edge_attr, 'W_f': W_f, 'b_f': b_f, 'W_s': W_s, 'b_s': b_s}
    _L3_gnn_all = _L3_gnn_setup()
    _L3_gnn_in = {k: v for k, v in _L3_gnn_all.items() if k in ('W_f', 'b_f', 'W_s', 'b_s')}
    del _L3_gnn_all
    return {'x': x, 'src': src, 'dst': dst, 'edge_attr_128': edge_attr_128, 'node_vec': node_vec, 'L0_gnn_W': _L0_gnn_in['W'], 'L0_gnn_b': _L0_gnn_in['b'], 'L0_gnn_agg_weight': _L0_gnn_in['agg_weight'], 'L1_gnn_W_homo': _L1_gnn_in['W_homo'], 'L1_gnn_b_homo': _L1_gnn_in['b_homo'], 'L1_gnn_W_hete': _L1_gnn_in['W_hete'], 'L1_gnn_b_hete': _L1_gnn_in['b_hete'], 'L1_gnn_W_self': _L1_gnn_in['W_self'], 'L1_gnn_b_self': _L1_gnn_in['b_self'], 'L2_gnn_W': _L2_gnn_in['W'], 'L2_gnn_b': _L2_gnn_in['b'], 'L3_gnn_W_f': _L3_gnn_in['W_f'], 'L3_gnn_b_f': _L3_gnn_in['b_f'], 'L3_gnn_W_s': _L3_gnn_in['W_s'], 'L3_gnn_b_s': _L3_gnn_in['b_s']}

def reference(x, src, dst, edge_attr_128, node_vec, L0_gnn_W, L0_gnn_b, L0_gnn_agg_weight, L1_gnn_W_homo, L1_gnn_b_homo, L1_gnn_W_hete, L1_gnn_b_hete, L1_gnn_W_self, L1_gnn_b_self, L2_gnn_W, L2_gnn_b, L3_gnn_W_f, L3_gnn_b_f, L3_gnn_W_s, L3_gnn_b_s):
    import jax
    import jax.numpy as jnp

    def _L0_gnn_ref(x, edge_index, W, b, agg_weight):
        import jax, jax.numpy as jnp
        import numpy as np
        N_NODES = 6250
        N_EDGES = 100000
        IN_CH = 128
        OUT_CH = 128
        row, col = (edge_index[0], edge_index[1])
        messages = jnp.einsum('ei,oi->eo', x[col], W) + b
        out = jax.ops.segment_sum(messages * agg_weight, row, num_segments=x.shape[0])
        return out

    def _L1_gnn_ref(feat, simi_weight, W_homo, b_homo, W_hete, b_hete, W_self, b_self, src_idx, dst_idx):
        import jax, jax.numpy as jnp
        import numpy as np
        N = 12500
        E = 200000
        D = 128
        NEG_SLOPE = 0.2

        def _edge_softmax(logits, dst, n):
            m = jax.ops.segment_max(logits, dst, num_segments=n)
            ex = jnp.exp(logits - m[dst])
            denom = jax.ops.segment_sum(ex, dst, num_segments=n)
            return ex / denom[dst]
        n = feat.shape[0]
        e = simi_weight[src_idx]
        lrelu = lambda x: jnp.where(x > 0, x, NEG_SLOPE * x)
        a_homo = _edge_softmax(lrelu(e), dst_idx, n)
        a_hete = _edge_softmax(lrelu(-e), dst_idx, n)
        mask = e > 0
        w_homo = jnp.where(mask, a_homo, 0.0)
        w_hete = jnp.where(mask, 0.0, a_hete)
        fsrc = feat[src_idx]
        neigh_homo = jax.ops.segment_sum(fsrc * w_homo[:, None], dst_idx, num_segments=n)
        neigh_hete = jax.ops.segment_sum(fsrc * w_hete[:, None], dst_idx, num_segments=n)
        h_neigh = neigh_homo @ W_homo + b_homo + (neigh_hete @ W_hete + b_hete)
        return feat @ W_self + b_self + h_neigh

    def _L2_gnn_ref(feats, W, b, src, dst):
        import jax, jax.numpy as jnp
        import numpy as np
        N = 12500
        E = 125000
        D = 128
        OUT = 128
        n = feats.shape[0]
        msg_sum = jax.ops.segment_sum(feats[src], dst, num_segments=n)
        deg = jax.ops.segment_sum(jnp.ones(src.shape, feats.dtype), dst, num_segments=n)
        h = msg_sum / jnp.maximum(deg, 1.0)[:, None]
        concat_ftrs = jnp.concatenate([feats, h, feats], axis=1)
        ftrs = jnp.tanh(concat_ftrs @ W.T + b)
        ftrs = ftrs / jnp.linalg.norm(ftrs)
        return ftrs

    def _L3_gnn_ref(x, edge_index, edge_attr, W_f, b_f, W_s, b_s):
        import jax, jax.numpy as jnp
        import numpy as np
        N_NODES = 6250
        N_EDGES = 100000
        C = 128
        D = 128
        Z = 2 * C + D
        src = edge_index[0]
        dst = edge_index[1]
        z = jnp.concatenate([x[dst], x[src], edge_attr], axis=-1)
        gate = jax.nn.sigmoid(z @ W_f + b_f)
        core = jax.nn.softplus(z @ W_s + b_s)
        msg = gate * core
        agg = jax.ops.segment_sum(msg, dst, num_segments=x.shape[0])
        return x + agg
    edge_index = jnp.stack([src, dst])
    x = _layernorm(x + _L0_gnn_ref(x, edge_index, L0_gnn_W, L0_gnn_b, L0_gnn_agg_weight), axis=-1)
    x = _layernorm(x + _L1_gnn_ref(x, node_vec, L1_gnn_W_homo, L1_gnn_b_homo, L1_gnn_W_hete, L1_gnn_b_hete, L1_gnn_W_self, L1_gnn_b_self, src, dst), axis=-1)
    x = _layernorm(x + _L2_gnn_ref(x, L2_gnn_W, L2_gnn_b, src, dst), axis=-1)
    x = _layernorm(x + _L3_gnn_ref(x, edge_index, edge_attr_128, L3_gnn_W_f, L3_gnn_b_f, L3_gnn_W_s, L3_gnn_b_s), axis=-1)
    return x

_drawn_inputs = setup_inputs


def setup_inputs(seed=0):
    import zlib

    import numpy as np

    out = dict(_drawn_inputs(seed))
    spreads = {'L1_gnn_b_homo': (0.0, 0.1), 'L1_gnn_b_hete': (0.0, 0.1), 'L1_gnn_b_self': (0.0, 0.1)}
    factors = {}
    for name, (base, spread) in spreads.items():
        noise = np.random.default_rng([zlib.crc32(name.encode()), seed]).standard_normal(out[name].shape)
        drawn = base * np.exp(spread * noise) if base else spread * noise
        out[name] = jnp.asarray(drawn.astype(out[name].dtype))
    for name, factor in factors.items():
        out[name] = (out[name] * factor).astype(out[name].dtype)
    return out
```

```python
import concourse.bass as bass
from concourse import mybir
from contextlib import ExitStack

F32 = mybir.dt.float32
BF16 = mybir.dt.bfloat16
I32 = mybir.dt.int32
ALU = mybir.AluOpType
ACT = mybir.ActivationFunctionType
AX = mybir.AxisListType
REDUCE_MAX = bass.bass_isa.ReduceOp.max
REDUCE_ADD = bass.bass_isa.ReduceOp.add

P = 128
D = 128
NODES = 6250
EDGES = 106250
WINDOWS = 50
NODES_PAD = WINDOWS * P
NOWHERE = NODES_PAD
TILES = -(-EDGES // P)
EMPTY_TILE = TILES
TILES_PAD = TILES + 1
TILE_ROWS = -(-TILES // P)
HALF = 4
STEPS = 2 * HALF
GROUPS_PER_PARTITION = 41
GROUPS_MAX = P * GROUPS_PER_PARTITION
assert GROUPS_MAX * STEPS >= TILES * WINDOWS + 2 * STEPS
TABLES = 4
SCATTER_ROWS = NODES_PAD + P
TILE_CODE = 64
FAR = 1000.0
EPS = 1e-5
SLOPE = 0.2
SOFT_RANGE = 60.0
LOWEST = -3.0e38


class Memory:

    def __init__(self, nc, ctx):
        def sb(name, shape, dtype=F32):
            return ctx.enter_context(nc.sbuf_tensor(name, shape, dtype))

        self.x_v = sb("x_v", [P, WINDOWS, D + 1])
        self.x = self.x_v[:, :, 0:D]
        self.v = self.x_v[:, :, D]
        self.acc = sb("acc", [P, WINDOWS, 2 * D])
        self.acc_small = sb("acc_small", [P, WINDOWS, 2])
        self.nodes = sb("nodes", [P, 51, 2 * D])
        self.src_i = sb("src_i", [P, TILES_PAD], I32)
        self.src_f = sb("src_f", [P, TILES_PAD])
        self.dst_f = sb("dst_f", [P, TILES_PAD])
        self.window_base = sb("window_base", [P, WINDOWS])
        self.column = sb("column", [P, P])
        self.lane = sb("lane", [P, 1])
        self.ident = sb("ident", [P, P])
        self.shift = sb("shift", [P, WINDOWS, 2])
        self.v_top = sb("v_top", [P, 2])
        self.groups = sb("groups", [P, 1], I32)
        self.wide_range = sb("wide_range", [P, 1], I32)
        self.agg = sb("agg", [P, 1])
        self.xt = sb("xt", [P, 2, 3, P])
        self.w0 = sb("w0", [P, D])
        self.w1 = sb("w1", [P, 3, D])
        self.w2 = sb("w2", [P, 3, D])
        self.w3 = sb("w3", [P, 3, 2 * D])
        self.b0 = sb("b0", [P, D])
        self.b1 = sb("b1", [P, 3, D])
        self.b2 = sb("b2", [P, D])
        self.b3 = sb("b3", [P, 2 * D])
        self.steps = nc.dram_tensor("steps", [GROUPS_MAX, 2 * STEPS], I32).ap()
        self.partial = [nc.dram_tensor(f"partial{i}", [SCATTER_ROWS, D], F32).ap() for i in range(TABLES)]
        self.x_rows = nc.dram_tensor("x_rows", [NODES_PAD, D + 1], F32).ap()
        self.b_rows = nc.dram_tensor("b_rows", [NODES_PAD, 2 * D], F32).ap()


def sems(nc, ctx, *names):
    return [ctx.enter_context(nc.semaphore(n)) for n in names]


def by_window(rows):
    return rows.rearrange("(w p) d -> p w d", p=P)


def step_registers(eng, mem, name, group, windows, tiles):
    w = t = None
    if windows and tiles:
        regs = [eng.alloc_register(f"{name}_step{u}") for u in range(2 * STEPS)]
        eng.load(regs, mem.steps[bass.ds(group, 1), :])
        w, t = regs[:STEPS], regs[STEPS:]
    elif windows:
        w = [eng.alloc_register(f"{name}_window{u}") for u in range(STEPS)]
        eng.load(w, mem.steps[bass.ds(group, 1), 0:STEPS])
    else:
        t = [eng.alloc_register(f"{name}_tile{u}") for u in range(STEPS)]
        eng.load(t, mem.steps[bass.ds(group, 1), STEPS:2 * STEPS])
    if w:
        w = [eng.snap(r, donate=True, min_val=0, max_val=WINDOWS - 1) for r in w]
    if t:
        t = [eng.snap(r, donate=True, min_val=0, max_val=TILES_PAD - 1) for r in t]
    return w, t


def group_count(eng, mem):
    return eng.value_load(mem.groups[0:1, 0:1], min_val=1, max_val=GROUPS_MAX - 2)


def phase_setup(nc, mem, a):
    with ExitStack() as ctx:
        def sb(name, shape, dtype=F32):
            return ctx.enter_context(nc.sbuf_tensor(name, shape, dtype))

        dst_i = sb("dst_i", [P, TILES_PAD], I32)
        lane_i = sb("lane_i", [P, 1], I32)
        column_i = sb("column_i", [P, P], I32)
        base_i = sb("base_i", [P, WINDOWS], I32)
        tile_i = sb("tile_i", [P, TILE_ROWS], I32)
        step_i = sb("step_i", [P, GROUPS_PER_PARTITION * STEPS], I32)
        tile_dst = sb("tile_dst", [P, TILE_ROWS, P], I32)
        v_in = sb("v_in", [P, WINDOWS])
        tile_no = sb("tile_no", [P, TILE_ROWS])
        lowest = sb("lowest", [P, TILE_ROWS])
        highest = sb("highest", [P, TILE_ROWS])
        low_side = sb("low_side", [P, WINDOWS, TILE_ROWS])
        high_side = sb("high_side", [P, WINDOWS, TILE_ROWS])
        first_last = sb("first_last", [P, 2 * WINDOWS + 2])
        over_all = sb("over_all", [P, 2 * WINDOWS + 2])
        count = sb("count", [P, WINDOWS])
        ended = sb("ended", [P, WINDOWS])
        jump = sb("jump", [P, WINDOWS])
        ones = sb("ones", [P, WINDOWS])
        step_f = sb("step_f", [P, GROUPS_PER_PARTITION * STEPS])
        code = sb("code", [P, GROUPS_PER_PARTITION * STEPS])
        part = sb("part", [P, GROUPS_PER_PARTITION * STEPS])
        code_i = sb("code_i", [P, GROUPS_PER_PARTITION * STEPS], I32)
        decoded = sb("decoded", [P, GROUPS_PER_PARTITION, 2, STEPS], I32)
        small = sb("small", [P, 4])
        (indices_in, tiles_in, nodes_in, const_made, link, edges_ready, all_reduced,
         zeros_made, steps_made, stored) = sems(
            nc, ctx, "indices_in", "tiles_in", "nodes_in", "const_made", "setup_link", "edges_ready",
            "all_reduced", "zeros_made", "steps_made", "setup_stored")

        with nc.Block() as block:
            @block.sync
            def _(sp):
                sp.dma_start(tile_dst[:], a["dst_tiles"]).then_inc(tiles_in, 16)
                sp.dma_start(v_in[:], a["node_vec_cols"]).then_inc(tiles_in, 16)
                sp.dma_start(mem.src_i[:], a["src_cols"]).then_inc(indices_in, 16)
                sp.dma_start(dst_i[:], a["dst_cols"]).then_inc(indices_in, 16)
                sp.dma_start(mem.x, by_window(a["x"])).then_inc(nodes_in, 16)
                sp.dma_start(mem.agg[:], a["L0_gnn_agg_weight"].broadcast_to([P, 1])).then_inc(nodes_in, 16)
                for dst, name in ((mem.w0, "L0_W"), (mem.w2, "L2_W"), (mem.w3, "L3_W")):
                    sp.dma_start(dst[:], a[name]).then_inc(nodes_in, 16)
                for j, name in enumerate(("homo", "hete", "self")):
                    sp.dma_start(mem.w1[:, j, :], a["L1_W_" + name]).then_inc(nodes_in, 16)
                    sp.dma_start(mem.b1[:, j, :], a["L1_b_" + name].broadcast_to([P, D])).then_inc(nodes_in, 16)
                for dst, name in ((mem.b0, "L0_b"), (mem.b2, "L2_b"), (mem.b3, "L3_b")):
                    sp.dma_start(dst[:], a[name].broadcast_to(list(dst.shape))).then_inc(nodes_in, 16)
                sp.wait_ge(zeros_made, 1)
                for table in mem.partial:
                    sp.dma_start(table.rearrange("(p r) d -> p (r d)", p=P),
                                 mem.nodes[:].rearrange("p w d -> p (w d)")[:, 0:SCATTER_ROWS // P * D]
                                 ).then_inc(stored, 16)
                sp.wait_ge(steps_made, 1)
                sp.dma_start(mem.steps.rearrange("(p g) s -> p (g s)", p=P),
                             decoded[:].rearrange("p g k s -> p (g k s)")).then_inc(stored, 16)
                sp.wait_ge(nodes_in, 16 * 14)
                sp.wait_ge(stored, 16 * (TABLES + 1))

            @block.gpsimd
            def _(pool):
                pool.iota(lane_i[:], [[0, 1]], base=0, channel_multiplier=1)
                pool.iota(column_i[:], [[1, P]], base=0, channel_multiplier=0)
                pool.iota(base_i[:], [[P, WINDOWS]], base=0, channel_multiplier=0)
                pool.iota(tile_i[:], [[P, TILE_ROWS]], base=0, channel_multiplier=1)
                pool.iota(step_i[:], [[1, GROUPS_PER_PARTITION * STEPS]], base=0,
                          channel_multiplier=GROUPS_PER_PARTITION * STEPS).then_inc(const_made, 1)
                pool.memset(mem.nodes[:], 0.0).then_inc(zeros_made, 1)
                pool.wait_ge(edges_ready, 1)
                pool.partition_all_reduce(over_all[:], first_last[:], P, REDUCE_MAX).then_inc(all_reduced, 1)

            @block.vector
            def _(dve):
                done = [0]

                def link_op(ins):
                    done[0] += 1
                    ins.then_inc(link, 1)
                    dve.wait_ge(link, done[0])

                dve.wait_ge(const_made, 1)
                nc.vector.tensor_copy(mem.lane[:], lane_i[:])
                nc.vector.tensor_copy(mem.column[:], column_i[:])
                nc.vector.tensor_copy(mem.window_base[:], base_i[:])
                nc.vector.tensor_copy(tile_no[:], tile_i[:])
                nc.vector.memset(ones[:], 1.0)
                link_op(nc.vector.tensor_copy(step_f[:], step_i[:]))
                nc.vector.tensor_scalar(mem.ident[:], mem.column[:], mem.lane[:], None, ALU.is_equal)
                dve.wait_ge(tiles_in, 32)
                nc.vector.tensor_reduce(lowest[:], tile_dst[:], AX.X, ALU.min)
                link_op(nc.vector.tensor_reduce(highest[:], tile_dst[:], AX.X, ALU.max))
                shape = [P, WINDOWS, TILE_ROWS]
                base = mem.window_base[:].unsqueeze(2).broadcast_to(shape)
                nc.vector.tensor_tensor(low_side[:], base, lowest[:].unsqueeze(1).broadcast_to(shape), ALU.subtract)
                link_op(nc.vector.tensor_tensor(high_side[:], highest[:].unsqueeze(1).broadcast_to(shape), base, ALU.subtract))
                link_op(nc.vector.tensor_scalar(high_side[:], high_side[:], 0.0, None, ALU.is_ge))
                link_op(nc.vector.scalar_tensor_tensor(low_side[:], low_side[:], float(1 - P), high_side[:],
                                                       ALU.is_ge, ALU.mult))
                tiles = tile_no[:].unsqueeze(1).broadcast_to(shape)
                link_op(nc.vector.scalar_tensor_tensor(high_side[:], tiles, 1.0, low_side[:], ALU.add, ALU.mult))
                link_op(nc.vector.tensor_scalar(tile_no[:], tile_no[:], -1.0, FAR, ALU.mult, ALU.add))
                link_op(nc.vector.tensor_tensor(low_side[:], low_side[:], tiles, ALU.mult))
                nc.vector.tensor_reduce(first_last[:, 0:WINDOWS], high_side[:], AX.X, ALU.max)
                nc.vector.tensor_reduce(first_last[:, WINDOWS:2 * WINDOWS], low_side[:], AX.X, ALU.max)
                link_op(nc.vector.tensor_scalar(count[:], v_in[:], -1.0, None, ALU.mult))
                nc.vector.tensor_reduce(first_last[:, 2 * WINDOWS:2 * WINDOWS + 1], v_in[:], AX.X, ALU.max)
                nc.vector.tensor_reduce(first_last[:, 2 * WINDOWS + 1:2 * WINDOWS + 2], count[:], AX.X,
                                        ALU.max).then_inc(edges_ready, 1)
                nc.vector.tensor_copy(mem.v, v_in[:])
                dve.wait_ge(indices_in, 32)
                nc.vector.tensor_copy(mem.src_f[:], mem.src_i[:])
                nc.vector.tensor_copy(mem.dst_f[:], dst_i[:])
                dve.wait_ge(all_reduced, 1)
                last1, far_first = over_all[:, 0:WINDOWS], over_all[:, WINDOWS:2 * WINDOWS]
                v_top = over_all[:, 2 * WINDOWS:2 * WINDOWS + 2]
                nc.vector.tensor_copy(mem.v_top[:], v_top)
                link_op(nc.vector.tensor_tensor(count[:], last1, far_first, ALU.add))
                link_op(nc.vector.tensor_scalar(jump[:], last1, 0.0, None, ALU.is_gt))
                link_op(nc.vector.scalar_tensor_tensor(count[:], count[:], -FAR, jump[:], ALU.add, ALU.mult))
                link_op(nc.vector.tensor_tensor_scan(ended[:], ones[:], count[:], 0.0, ALU.mult, ALU.add))
                link_op(nc.vector.tensor_tensor(count[:], count[:], ended[:], ALU.subtract))
                link_op(nc.vector.tensor_tensor(count[:], count[:], far_first, ALU.subtract))
                link_op(nc.vector.tensor_scalar(count[:], count[:], FAR, None, ALU.add))
                link_op(nc.vector.tensor_tensor(jump[:, 0:WINDOWS - 1], count[:, 1:WINDOWS], count[:, 0:WINDOWS - 1],
                                                ALU.subtract))
                link_op(nc.vector.tensor_scalar(jump[:, 0:WINDOWS - 1], jump[:, 0:WINDOWS - 1], float(TILE_CODE), 1.0,
                                                ALU.mult, ALU.add))
                link_op(nc.vector.tensor_scalar(code[:], step_f[:], count[:, 0:1], float(TILE_CODE),
                                                ALU.add, ALU.mult))
                for w in range(WINDOWS - 1):
                    link_op(nc.vector.tensor_scalar(part[:], step_f[:], ended[:, w:w + 1], jump[:, w:w + 1],
                                                    ALU.is_ge, ALU.mult))
                    link_op(nc.vector.tensor_tensor(code[:], code[:], part[:], ALU.add))
                total = ended[:, WINDOWS - 1:WINDOWS]
                link_op(nc.vector.scalar_tensor_tensor(code[:], step_f[:], total, code[:], ALU.is_lt, ALU.mult))
                link_op(nc.vector.tensor_scalar(part[:], step_f[:], total, float(TILE_CODE * EMPTY_TILE + WINDOWS - 1),
                                                ALU.is_ge, ALU.mult))
                link_op(nc.vector.tensor_tensor(code_i[:], code[:], part[:], ALU.add))
                coded = code_i[:].rearrange("p (g s) -> p g s", s=STEPS)
                nc.vector.tensor_scalar(decoded[:, :, 0, :], coded, TILE_CODE - 1, None, ALU.bitwise_and)
                nc.vector.tensor_scalar(decoded[:, :, 1, :], coded, 6, None,
                                        ALU.logical_shift_right).then_inc(steps_made, 1)
                link_op(nc.vector.tensor_scalar(small[:, 0:1], total, float(STEPS - 1), float(STEPS), ALU.add, ALU.max))
                link_op(nc.vector.tensor_copy(mem.groups[:], small[:, 0:1]))
                nc.vector.tensor_scalar(mem.groups[:], mem.groups[:], 3, None, ALU.logical_shift_right)
                link_op(nc.vector.tensor_tensor(small[:, 1:2], mem.v_top[:, 0:1], mem.v_top[:, 1:2], ALU.add))
                link_op(nc.vector.tensor_scalar(small[:, 1:2], small[:, 1:2], SOFT_RANGE, None, ALU.is_le))
                link_op(nc.vector.tensor_scalar(mem.wide_range[:], small[:, 1:2], -1.0, 1.0, ALU.mult, ALU.add))
                link_op(nc.vector.scalar_tensor_tensor(small[:, 2:4], mem.v_top[:], SLOPE, mem.v_top[:],
                                                       ALU.mult, ALU.max))
                nc.vector.tensor_copy(mem.shift[:], small[:, 2:4].unsqueeze(1).broadcast_to([P, WINDOWS, 2]))


def phase_project(nc, mem, name, sources, weights, width, finish, prepare=None):
    with ExitStack() as ctx:
        def ps(tag, shape):
            return [ctx.enter_context(nc.psum_tensor(f"{name}_{tag}{s}", shape, F32)) for s in range(2)]

        turned, sums = ps("turned", [P, len(sources), P]), ps("sums", [P, width])
        staged = ctx.enter_context(nc.sbuf_tensor(f"{name}_staged", [P, 2, len(sources), P], F32))
        transposed, copied, summed, sums_free, prepared, staged_in, staged_free, turn = sems(
            nc, ctx, *(f"{name}_{s}" for s in (
                "transposed", "copied", "summed", "sums_free", "prepared", "staged_in", "staged_free", "turn")))
        with nc.Block() as block:
            @block.gpsimd
            def _(pool):
                pool.wait_ge(prepared, 1)
                with pool.Fori(0, WINDOWS // 2) as i:
                    for s in range(2):
                        pool.wait_ge(staged_free, 2 * i + s + 1)
                        pool.sem_inc(turn, 1)
                        for j, source in enumerate(sources):
                            last = pool.tensor_copy(staged[:, s, j:j + 1, :], source[:, bass.ds(2 * i + s, 1), :])
                        last.then_inc(staged_in, 1)

            @block.tensor
            def _(pe):
                pe.sem_inc(staged_free, 2)
                with pe.Fori(0, WINDOWS // 2) as i:
                    for s in range(2):
                        pe.wait_ge(staged_in, 2 * i + s + 1)
                        for j in range(len(sources)):
                            last = nc.tensor.transpose(turned[s][:, j, :], staged[:, s, j, :], mem.ident[:])
                        last.then_inc(transposed, 1)
                    for s in range(2):
                        pe.wait_ge(copied, 2 * i + s + 1)
                        pe.wait_ge(sums_free, 2 * i + s + 1)
                        for j, weight in enumerate(weights):
                            last = nc.tensor.matmul(sums[s][:], mem.xt[:, s, j, :], weight,
                                                    start=(j == 0), stop=(j == len(weights) - 1))
                        last.then_inc(summed, 1)

            @block.scalar
            def _(act):
                with act.Fori(0, WINDOWS // 2) as i:
                    for s in range(2):
                        act.wait_ge(transposed, 2 * i + s + 1)
                        act.sem_inc(staged_free, 1)
                        nc.scalar.activation(mem.xt[:, s, 0:len(sources), :], turned[s][:],
                                             ACT.Copy).then_inc(copied, 1)

            @block.vector
            def _(dve):
                if prepare:
                    prepare(dve)
                dve.sem_inc(prepared, 1)
                dve.sem_inc(sums_free, 2)
                with dve.Fori(0, WINDOWS // 2) as i:
                    for s in range(2):
                        dve.wait_ge(summed, 2 * i + s + 1)
                        finish(dve, 2 * i + s, s, sums[s]).then_inc(sums_free, 1)


CHUNK = 10


def phase_norm(nc, mem, name, before, store):
    chunks = [slice(c, c + CHUNK) for c in range(0, WINDOWS, CHUNK)]
    with ExitStack() as ctx:
        total = ctx.enter_context(nc.sbuf_tensor(f"{name}_total", [P, WINDOWS], F32))
        mean = ctx.enter_context(nc.sbuf_tensor(f"{name}_mean", [P, WINDOWS], F32))
        square = ctx.enter_context(nc.sbuf_tensor(f"{name}_square", [P, WINDOWS], F32))
        var = ctx.enter_context(nc.sbuf_tensor(f"{name}_var", [P, WINDOWS], F32))
        sigma = ctx.enter_context(nc.sbuf_tensor(f"{name}_sigma", [P, WINDOWS], F32))
        scale = ctx.enter_context(nc.sbuf_tensor(f"{name}_scale", [P, WINDOWS], F32))
        squares = mem.acc[:, :, 0:D]
        step, centred, squared, var_made, sigma_made, normed, stored = sems(
            nc, ctx, *(f"{name}_{s}" for s in (
                "step", "centred", "squared", "var_made", "sigma_made", "normed", "stored")))
        shape = [P, CHUNK, D]
        with nc.Block() as block:
            @block.vector
            def _(dve):
                before(dve)
                for n, c in enumerate(chunks):
                    nc.vector.tensor_reduce(total[:, c], mem.x[:, c, :], AX.X, ALU.add).then_inc(step, 1)
                    dve.wait_ge(step, 2 * n + 1)
                    nc.vector.tensor_scalar(mean[:, c], total[:, c], 1.0 / D, None, ALU.mult).then_inc(step, 1)
                    dve.wait_ge(step, 2 * n + 2)
                    nc.vector.tensor_tensor(mem.x[:, c, :], mem.x[:, c, :],
                                            mean[:, c].unsqueeze(2).broadcast_to(shape),
                                            ALU.subtract).then_inc(centred, 1)
                for n, c in enumerate(chunks):
                    dve.wait_ge(squared, n + 1)
                    last = nc.vector.tensor_reduce(square[:, c], squares[:, c, :], AX.X, ALU.add)
                base = 2 * len(chunks)
                last.then_inc(step, 1)
                dve.wait_ge(step, base + 1)
                nc.vector.tensor_scalar(var[:], square[:], 1.0 / D, EPS, ALU.mult, ALU.add).then_inc(var_made, 1)
                dve.wait_ge(sigma_made, 1)
                nc.vector.reciprocal(scale[:], sigma[:]).then_inc(step, 1)
                dve.wait_ge(step, base + 2)
                for c in chunks:
                    nc.vector.tensor_tensor(mem.x[:, c, :], mem.x[:, c, :],
                                            scale[:, c].unsqueeze(2).broadcast_to(shape),
                                            ALU.mult).then_inc(normed, 1)

            @block.scalar
            def _(act):
                for n, c in enumerate(chunks):
                    act.wait_ge(centred, n + 1)
                    nc.scalar.activation(squares[:, c, :], mem.x[:, c, :], ACT.Square).then_inc(squared, 1)
                act.wait_ge(var_made, 1)
                nc.scalar.activation(sigma[:], var[:], ACT.Sqrt).then_inc(sigma_made, 1)

            @block.sync
            def _(sp):
                sent = 0
                rows, with_v = store
                for n, c in enumerate(chunks):
                    sp.wait_ge(normed, n + 1)
                    first, end = c.start * P, min(c.stop * P, rows.shape[0])
                    whole = (end - first) // P
                    source = mem.x_v if with_v else mem.x
                    sp.dma_start(by_window(rows[first:first + whole * P, :]),
                                 source[:, c.start:c.start + whole, :]).then_inc(stored, 16)
                    sent += 1
                    if first + whole * P < end:
                        rest = end - first - whole * P
                        sp.dma_start(rows[first + whole * P:end, :],
                                     source[0:rest, c.start + whole, :]).then_inc(stored, 16)
                        sent += 1
                        break
                sp.wait_ge(stored, 16 * sent)


def phase_scatter(nc, mem, src_rows):
    with ExitStack() as ctx:
        def sb(name, shape, dtype=F32):
            return ctx.enter_context(nc.sbuf_tensor(name, shape, dtype))

        def pair(name):
            return [ctx.enter_context(nc.psum_tensor(f"{name}{h}", [P, HALF, P], F32)) for h in range(2)]

        earlier = sb("s0_earlier", [P, P])
        to_trash = sb("s0_to_trash", [P, TILES_PAD])
        sources = sb("s0_sources", [P, STEPS, P], I32)
        into = sb("s0_into", [P, STEPS, P], BF16)
        same = sb("s0_same", [P, STEPS, P], BF16)
        junk = sb("s0_junk", [P, STEPS, P], BF16)
        before = sb("s0_before", [P, STEPS])
        repeat = sb("s0_repeat", [P, STEPS])
        rows = sb("s0_rows", [P, STEPS], I32)
        primer = sb("s0_primer", [1, 2 * TABLES, P], I32)
        mix = sb("s0_mix", [P, STEPS, P])
        tile = sb("s0_tile", [P, STEPS, D])
        mix_ps, tile_ps = pair("s0_mix_ps"), pair("s0_tile_ps")
        (set_up, sources_free, onehots_free, onehots, counted, repeat_made, rows_made, mixed, mix_copied,
         tile_summed, tile_copied) = sems(nc, ctx, *("s0_" + n for n in (
             "set_up", "sources_free", "onehots_free", "onehots", "counted", "repeat_made", "rows_made",
             "mixed", "mix_copied", "tile_summed", "tile_copied")))
        sources_in = sems(nc, ctx, "s0_sources_in0", "s0_sources_in1")
        added = sems(nc, ctx, *(f"s0_added{i}" for i in range(TABLES)))
        turn = sems(nc, ctx, "s0_turn")[0]
        with nc.Block() as block:
            @block.sync
            def _(sp):
                n = group_count(sp, mem)
                with sp.Fori(0, n) as g:
                    _, t = step_registers(sp, mem, "s0_sp", g, False, True)
                    for h in range(2):
                        sp.wait_ge(sources_free, 2 * g + h + 1)
                        for i in range(HALF):
                            u = HALF * h + i
                            sp.dma_start(sources[:, u, :], src_rows[bass.ds(t[u], 1), :].broadcast_to([P, P])
                                         ).then_inc(sources_in[h], 16)

            @block.vector
            def _(dve):
                nc.vector.tensor_scalar(earlier[:], mem.column[:], mem.lane[:], None, ALU.is_lt)
                nc.vector.tensor_scalar(to_trash[:], mem.src_f[:], -1.0, float(NODES_PAD),
                                        ALU.mult, ALU.add).then_inc(set_up, 1)
                dve.wait_ge(set_up, 1)
                nc.vector.tensor_scalar(to_trash[:], to_trash[:], mem.lane[:], None, ALU.add).then_inc(set_up, 1)
                dve.wait_ge(set_up, 2)
                dve.sem_inc(sources_free, 2)
                n = group_count(dve, mem)
                with dve.Fori(0, n) as g:
                    w, t = step_registers(dve, mem, "s0_dve", g, True, True)
                    for h in range(2):
                        dve.wait_ge(onehots_free, 2 * g + h + 1)
                        for i in range(HALF):
                            u = HALF * h + i
                            nc.vector.tensor_scalar(into[:, u, :], mem.column[:], mem.window_base[:, bass.ds(w[u], 1)],
                                                    mem.dst_f[:, bass.ds(t[u], 1)], ALU.add, ALU.is_equal)
                        dve.wait_ge(sources_in[h], 16 * HALF * (g + 1))
                        for i in range(HALF):
                            u = HALF * h + i
                            last = nc.vector.tensor_scalar(same[:, u, :], sources[:, u, :],
                                                           mem.src_f[:, bass.ds(t[u], 1)], None, ALU.is_equal)
                        last.then_inc(onehots, 1)
                        for i in range(HALF):
                            u = HALF * h + i
                            last = nc.vector.scalar_tensor_tensor(junk[:, u, :], sources[:, u, :],
                                                                  mem.src_f[:, bass.ds(t[u], 1)], earlier[:],
                                                                  ALU.is_equal, ALU.mult, accum_out=before[:, u:u + 1])
                        last.then_inc(counted, 1)
                        dve.wait_ge(counted, 2 * g + h + 1)
                        dve.sem_inc(sources_free, 1)
                        b = slice(HALF * h, HALF * h + HALF)
                        nc.vector.tensor_scalar(repeat[:, b], before[:, b], 0.0, None, ALU.is_gt).then_inc(repeat_made, 1)
                        dve.wait_ge(repeat_made, 2 * g + h + 1)
                        for i in range(TABLES):
                            dve.wait_ge(added[i], 16 * (2 * g + h) + 16)
                        for i in range(HALF):
                            u = HALF * h + i
                            last = nc.vector.tensor_scalar(rows[:, u:u + 1], repeat[:, u:u + 1],
                                                           to_trash[:, bass.ds(t[u], 1)],
                                                           mem.src_f[:, bass.ds(t[u], 1)], ALU.mult, ALU.add)
                        last.then_inc(rows_made, 1)

            @block.tensor
            def _(pe):
                pe.sem_inc(onehots_free, 2)
                n = group_count(pe, mem)
                with pe.Fori(0, n) as g:
                    w, _ = step_registers(pe, mem, "s0_pe", g, True, False)
                    for h in range(2):
                        pe.wait_ge(onehots, 2 * g + h + 1)
                        for i in range(HALF):
                            last = nc.tensor.matmul(mix_ps[h][:, i, :], into[:, HALF * h + i, :],
                                                    same[:, HALF * h + i, :], start=True, stop=True)
                        last.then_inc(mixed, 1)
                    for h in range(2):
                        pe.wait_ge(mix_copied, 2 * g + h + 1)
                        pe.sem_inc(onehots_free, 1)
                        for i in range(HALF):
                            u = HALF * h + i
                            last = nc.tensor.matmul(
                                tile_ps[h][:, i, :], mix[:, u, :],
                                mem.nodes[:, bass.ds(w[u], 1), 0:D].rearrange("p a b -> p (a b)"), start=True, stop=True)
                        last.then_inc(tile_summed, 1)

            @block.scalar
            def _(act):
                n = group_count(act, mem)
                with act.Fori(0, n) as g:
                    for h in range(2):
                        b = slice(HALF * h, HALF * h + HALF)
                        act.wait_ge(mixed, 2 * g + h + 1)
                        nc.scalar.activation(mix[:, b, :], mix_ps[h][:], ACT.Copy).then_inc(mix_copied, 1)
                    for h in range(2):
                        b = slice(HALF * h, HALF * h + HALF)
                        act.wait_ge(tile_summed, 2 * g + h + 1)
                        for i in range(TABLES):
                            act.wait_ge(added[i], 16 * (2 * g + h) + 16)
                        nc.scalar.activation(tile[:, b, :], tile_ps[h][:], ACT.Copy).then_inc(tile_copied, 1)

            @block.gpsimd
            def _(pool):
                for k in range(2):
                    for i in range(TABLES):
                        pool.dma_start(primer[0:1, 2 * i + k, :], src_rows[0:1, :]).then_inc(added[i], 16)
                    for i in range(TABLES):
                        pool.wait_ge(added[i], 16 * (k + 1))
                n = group_count(pool, mem)
                with pool.Fori(0, n) as g:
                    for h in range(2):
                        pool.wait_ge(rows_made, 2 * g + h + 1)
                        pool.wait_ge(tile_copied, 2 * g + h + 1)
                        pool.sem_inc(turn, 1)
                        for i in range(HALF):
                            u = HALF * h + i
                            pool.wait_ge(added[i], 16 * (2 * g + h) + 32)
                            pool.sem_inc(turn, 1)
                            pool.indirect_dma_start(
                                mem.partial[i], bass.IndirectOffsetOnAxis(ap=rows[:, u:u + 1], axis=0),
                                tile[:, u, :], None, compute_op=ALU.add).then_inc(added[i], 16)
                for i in range(TABLES):
                    pool.wait_ge(added[i], 16 * (2 * n) + 32)


def gather_loop(pool, mem, table, rows, index, index_in, rows_free, turn, rows_in):
    n = group_count(pool, mem)
    with pool.Fori(0, n) as g:
        for h in range(2):
            pool.wait_ge(index_in, 2 * g + h + 1)
            pool.wait_ge(rows_free, 2 * g + h + 1)
            pool.sem_inc(turn, 1)
            for u in range(HALF * h, HALF * h + HALF):
                pool.indirect_dma_start(rows[:, u, :], None, table,
                                        bass.IndirectOffsetOnAxis(ap=index[:, u:u + 1], axis=0)
                                        ).then_inc(rows_in[h], 16)


def copy_indices(nc, mem, index, h, tiles):
    for u in range(HALF * h, HALF * h + HALF):
        last = nc.scalar.activation(index[:, u:u + 1], mem.src_i[:, bass.ds(tiles[u], 1)], ACT.Copy)
    return last


def build_onehots(nc, mem, into, h, w, t):
    for u in range(HALF * h, HALF * h + HALF):
        last = nc.vector.tensor_scalar(into[:, u, :], mem.column[:], mem.window_base[:, bass.ds(w[u], 1)],
                                       mem.dst_f[:, bass.ds(t[u], 1)], ALU.add, ALU.is_equal)
    return last


def window(ap, w):
    return ap[:, bass.ds(w, 1), :].rearrange("p a b -> p (a b)")


def phase_attend(nc, mem):
    with ExitStack() as ctx:
        def sb(name, shape, dtype=F32):
            return ctx.enter_context(nc.sbuf_tensor("s1_" + name, shape, dtype))

        def ps(name, shape):
            return ctx.enter_context(nc.psum_tensor("s1_" + name, shape, F32))

        index = sb("index", [P, STEPS], I32)
        rows = sb("rows", [P, STEPS, D + 1])
        into = sb("into", [P, STEPS, P])
        into_t = sb("into_t", [P, STEPS, P])
        minus_v = sb("minus_v", [P, STEPS])
        logits = sb("logits", [P, STEPS, 2])
        shifted = sb("shifted", [P, STEPS, 2])
        weight = sb("weight", [P, STEPS, 2])
        taken = sb("taken", [P, STEPS, 2])
        weighted = sb("weighted", [P, STEPS, 2 * D])
        into_t_ps = [ps(f"into_t_ps{h}", [P, HALF, P]) for h in range(2)]
        shift_ps = [into_t_ps[h][:].rearrange("p i (e k) -> p i e k", k=2)[:, :, 0, :] for h in range(2)]
        sums_ps = [[ps(f"sums_ps{h}{k}", [P, 2, 2 * D]) for k in range(2)] for h in range(2)]
        weights_ps = [ps(f"weights_ps{h}", [P, HALF, 2]) for h in range(2)]
        (index_in, rows_free, turn, onehots_free, onehots, turned, turned_copied, shifts, negated, logits_made,
         shifted_made, weights_made, taken_made, homo_made, hete_made, summed, added) = sems(
            nc, ctx, *("s1_" + n for n in (
                "index_in", "rows_free", "turn", "onehots_free", "onehots", "turned", "turned_copied", "shifts",
                "negated", "logits_made", "shifted_made", "weights_made", "taken_made", "homo_made", "hete_made",
                "summed", "added")))
        rows_in = sems(nc, ctx, "s1_rows_in0", "s1_rows_in1")
        with nc.Block() as block:
            @block.gpsimd
            def _(pool):
                gather_loop(pool, mem, mem.x_rows, rows, index, index_in, rows_free, turn, rows_in)

            @block.scalar
            def _(act):
                _, t = step_registers(act, mem, "s1_first", 0, False, True)
                for h in range(2):
                    copy_indices(nc, mem, index, h, t).then_inc(index_in, 1)
                n = group_count(act, mem)
                with act.Fori(0, n) as g:
                    _, t = step_registers(act, mem, "s1_act", g + 1, False, True)
                    for h in range(2):
                        act.wait_ge(turned, 2 * g + h + 1)
                        nc.scalar.activation(into_t[:, HALF * h:HALF * h + HALF, :], into_t_ps[h][:],
                                             ACT.Copy).then_inc(turned_copied, 1)
                    for h in range(2):
                        b = slice(HALF * h, HALF * h + HALF)
                        act.wait_ge(rows_in[h], 16 * HALF * (g + 1))
                        copy_indices(nc, mem, index, h, t).then_inc(index_in, 1)
                        act.wait_ge(shifted_made, 2 * g + h + 1)
                        nc.scalar.activation(weight[:, b, :], shifted[:, b, :], ACT.Exp).then_inc(weights_made, 1)
                        act.wait_ge(taken_made, 2 * g + h + 1)
                        for u in range(HALF * h, HALF * h + HALF):
                            last = nc.scalar.activation(weighted[:, u, 0:D], rows[:, u, 0:D], ACT.Copy,
                                                        scale=taken[:, u, 0:1])
                        last.then_inc(homo_made, 1)

            @block.vector
            def _(dve):
                nc.vector.memset(mem.acc[:], 0.0)
                nc.vector.memset(mem.acc_small[:], 0.0).then_inc(added, 1)
                n = group_count(dve, mem)
                with dve.Fori(0, n) as g:
                    w, t = step_registers(dve, mem, "s1_dve", g, True, True)
                    for h in range(2):
                        dve.wait_ge(onehots_free, 2 * g + h + 1)
                        build_onehots(nc, mem, into, h, w, t).then_inc(onehots, 1)
                    for h in range(2):
                        b = slice(HALF * h, HALF * h + HALF)
                        j = 2 * g + h + 1
                        v = rows[:, b, D]
                        dve.wait_ge(rows_in[h], 16 * HALF * (g + 1))
                        nc.vector.tensor_scalar(minus_v[:, b], v, -1.0, None, ALU.mult).then_inc(negated, 1)
                        nc.vector.scalar_tensor_tensor(logits[:, b, 0], v, SLOPE, v, ALU.mult, ALU.max)
                        dve.wait_ge(negated, j)
                        nc.vector.scalar_tensor_tensor(logits[:, b, 1], minus_v[:, b], SLOPE, minus_v[:, b],
                                                       ALU.mult, ALU.max).then_inc(logits_made, 1)
                        dve.wait_ge(logits_made, j)
                        dve.wait_ge(shifts, j)
                        nc.vector.tensor_tensor(shifted[:, b, :], logits[:, b, :], shift_ps[h],
                                                ALU.subtract).then_inc(shifted_made, 1)
                        dve.wait_ge(weights_made, j)
                        nc.vector.scalar_tensor_tensor(taken[:, b, 0], v, 0.0, weight[:, b, 0], ALU.is_gt, ALU.mult)
                        nc.vector.scalar_tensor_tensor(taken[:, b, 1], v, 0.0, weight[:, b, 1],
                                                       ALU.is_le, ALU.mult).then_inc(taken_made, 1)
                        dve.wait_ge(taken_made, j)
                        for u in range(HALF * h, HALF * h + HALF):
                            last = nc.vector.tensor_scalar(weighted[:, u, D:2 * D], rows[:, u, 0:D],
                                                           taken[:, u, 1:2], None, ALU.mult)
                        last.then_inc(hete_made, 1)
                    for h in range(2):
                        dve.wait_ge(summed, 2 * g + h + 1)
                        for i in range(HALF):
                            u = HALF * h + i
                            dve.wait_ge(added, STEPS * g + u + 1)
                            acc, small = window(mem.acc, w[u]), window(mem.acc_small, w[u])
                            nc.vector.tensor_tensor(acc, acc, sums_ps[h][i // 2][:, i % 2, :], ALU.add)
                            nc.vector.tensor_tensor(small, small, weights_ps[h][:, u % HALF, :], ALU.add).then_inc(added, 1)

            @block.tensor
            def _(pe):
                pe.sem_inc(onehots_free, 2)
                pe.sem_inc(rows_free, 2)
                n = group_count(pe, mem)
                with pe.Fori(0, n) as g:
                    w, _ = step_registers(pe, mem, "s1_pe", g, True, False)
                    for h in range(2):
                        pe.wait_ge(onehots, 2 * g + h + 1)
                        for i in range(HALF):
                            last = nc.tensor.transpose(into_t_ps[h][:, i, :], into[:, HALF * h + i, :], mem.ident[:])
                        last.then_inc(turned, 1)
                    for h in range(2):
                        pe.wait_ge(turned_copied, 2 * g + h + 1)
                        for u in range(HALF * h, HALF * h + HALF):
                            last = nc.tensor.matmul(shift_ps[h][:, u % HALF, :], into_t[:, u, :], window(mem.shift, w[u]),
                                                    start=True, stop=True)
                        last.then_inc(shifts, 1)
                    for h in range(2):
                        pe.wait_ge(homo_made, 2 * g + h + 1)
                        pe.wait_ge(hete_made, 2 * g + h + 1)
                        pe.wait_ge(added, STEPS * g + 1)
                        for i in range(HALF):
                            u = HALF * h + i
                            nc.tensor.matmul(sums_ps[h][i // 2][:, i % 2, :], into[:, u, :], weighted[:, u, :],
                                             start=True, stop=True)
                            last = nc.tensor.matmul(weights_ps[h][:, u % HALF, :], into[:, u, :], weight[:, u, :],
                                                    start=True, stop=True)
                        last.then_inc(summed, 1)
                        pe.wait_ge(summed, 2 * g + h + 1)
                        pe.sem_inc(onehots_free, 1)
                        pe.sem_inc(rows_free, 1)


def phase_mean(nc, mem):
    with ExitStack() as ctx:
        def sb(name, shape, dtype=F32):
            return ctx.enter_context(nc.sbuf_tensor("s2_" + name, shape, dtype))

        def ps(name, shape):
            return ctx.enter_context(nc.psum_tensor("s2_" + name, shape, F32))

        index = sb("index", [P, STEPS], I32)
        rows = sb("rows", [P, STEPS, D + 1])
        into = sb("into", [P, STEPS, P])
        one = sb("one", [P, 2])
        sums_ps = [ps(f"sums_ps{h}", [P, HALF, D]) for h in range(2)]
        degree_ps = [ps(f"degree_ps{h}", [P, HALF, 2]) for h in range(2)]
        (index_in, rows_free, turn, onehots_free, onehots, summed, added, one_made) = sems(
            nc, ctx, *("s2_" + n for n in (
                "index_in", "rows_free", "turn", "onehots_free", "onehots", "summed", "added", "one_made")))
        rows_in = sems(nc, ctx, "s2_rows_in0", "s2_rows_in1")
        with nc.Block() as block:
            @block.gpsimd
            def _(pool):
                gather_loop(pool, mem, mem.x_rows, rows, index, index_in, rows_free, turn, rows_in)

            @block.scalar
            def _(act):
                _, t = step_registers(act, mem, "s2_first", 0, False, True)
                for h in range(2):
                    copy_indices(nc, mem, index, h, t).then_inc(index_in, 1)
                n = group_count(act, mem)
                with act.Fori(0, n) as g:
                    _, t = step_registers(act, mem, "s2_act", g + 1, False, True)
                    for h in range(2):
                        act.wait_ge(rows_in[h], 16 * HALF * (g + 1))
                        copy_indices(nc, mem, index, h, t).then_inc(index_in, 1)

            @block.vector
            def _(dve):
                nc.vector.memset(one[:], 1.0).then_inc(one_made, 1)
                nc.vector.memset(mem.acc[:, :, 0:D], 0.0)
                nc.vector.memset(mem.acc_small[:], 0.0).then_inc(added, 1)
                n = group_count(dve, mem)
                with dve.Fori(0, n) as g:
                    w, t = step_registers(dve, mem, "s2_dve", g, True, True)
                    for h in range(2):
                        dve.wait_ge(onehots_free, 2 * g + h + 1)
                        build_onehots(nc, mem, into, h, w, t).then_inc(onehots, 1)
                    for h in range(2):
                        dve.wait_ge(summed, 2 * g + h + 1)
                        for i in range(HALF):
                            u = HALF * h + i
                            dve.wait_ge(added, STEPS * g + u + 1)
                            acc, small = window(mem.acc[:, :, 0:D], w[u]), window(mem.acc_small, w[u])
                            nc.vector.tensor_tensor(acc, acc, sums_ps[h][:, i, :], ALU.add)
                            nc.vector.tensor_tensor(small, small, degree_ps[h][:, i, :], ALU.add).then_inc(added, 1)

            @block.tensor
            def _(pe):
                pe.sem_inc(onehots_free, 2)
                pe.sem_inc(rows_free, 2)
                pe.wait_ge(one_made, 1)
                n = group_count(pe, mem)
                with pe.Fori(0, n) as g:
                    for h in range(2):
                        pe.wait_ge(onehots, 2 * g + h + 1)
                        pe.wait_ge(rows_in[h], 16 * HALF * (g + 1))
                        pe.wait_ge(added, STEPS * g + 1)
                        for i in range(HALF):
                            u = HALF * h + i
                            nc.tensor.matmul(sums_ps[h][:, i, :], into[:, u, :], rows[:, u, 0:D],
                                             start=True, stop=True)
                            last = nc.tensor.matmul(degree_ps[h][:, i, :], into[:, u, :], one[:], start=True, stop=True)
                        last.then_inc(summed, 1)
                        pe.wait_ge(summed, 2 * g + h + 1)
                        pe.sem_inc(onehots_free, 1)
                        pe.sem_inc(rows_free, 1)


SOFT_TOP = 30.0


def phase_gate(nc, mem, edge_attr):
    with ExitStack() as ctx:
        def sb(name, shape, dtype=F32):
            return ctx.enter_context(nc.sbuf_tensor("s3_" + name, shape, dtype))

        def ps(name, shape):
            return ctx.enter_context(nc.psum_tensor("s3_" + name, shape, F32))

        index = sb("index", [P, STEPS], I32)
        rows = sb("rows", [P, STEPS, 2 * D])
        into = sb("into", [P, STEPS, P])
        into_t = sb("into_t", [P, STEPS, P])
        edge = sb("edge", [P, STEPS, P])
        logits = sb("logits", [P, STEPS, 2 * D])
        soft = mem.acc[:, 0:STEPS, D:2 * D]
        into_t_ps = [ps(f"into_t_ps{h}", [P, HALF, P]) for h in range(2)]
        logits_ps = [[ps(f"logits_ps{h}{k}", [P, 2, 2 * D]) for k in range(2)] for h in range(2)]
        sums_ps = [ps(f"sums_ps{h}", [P, HALF, D]) for h in range(2)]
        (index_in, rows_free, turn, onehots_free, onehots, turned, turned_copied, edge_free, products, logits_made,
         capped, exp_made, log_made, gate_exp, gate_one, gate_made, core_made, messages, summed, added) = sems(
            nc, ctx, *("s3_" + n for n in (
                "index_in", "rows_free", "turn", "onehots_free", "onehots", "turned", "turned_copied", "edge_free",
                "products", "logits_made", "capped", "exp_made", "log_made", "gate_exp", "gate_one", "gate_made",
                "core_made", "messages", "summed", "added")))
        rows_in = sems(nc, ctx, "s3_rows_in0", "s3_rows_in1")
        edge_in = sems(nc, ctx, "s3_edge_in0", "s3_edge_in1")
        with nc.Block() as block:
            @block.gpsimd
            def _(pool):
                gather_loop(pool, mem, mem.b_rows, rows, index, index_in, rows_free, turn, rows_in)

            @block.sync
            def _(sp):
                n = group_count(sp, mem)
                with sp.Fori(0, n) as g:
                    _, t = step_registers(sp, mem, "s3_sp", g, False, True)
                    for h in range(2):
                        sp.wait_ge(edge_free, 2 * g + h + 1)
                        for u in range(HALF * h, HALF * h + HALF):
                            sp.dma_start(edge[:, u, :], edge_attr[:, bass.ds(t[u] * P, P)]).then_inc(edge_in[h], 16)

            @block.scalar
            def _(act):
                _, t = step_registers(act, mem, "s3_first", 0, False, True)
                for h in range(2):
                    copy_indices(nc, mem, index, h, t).then_inc(index_in, 1)
                n = group_count(act, mem)
                with act.Fori(0, n) as g:
                    _, t = step_registers(act, mem, "s3_act", g + 1, False, True)
                    for h in range(2):
                        act.wait_ge(turned, 2 * g + h + 1)
                        nc.scalar.activation(into_t[:, HALF * h:HALF * h + HALF, :], into_t_ps[h][:],
                                             ACT.Copy).then_inc(turned_copied, 1)
                    for h in range(2):
                        b = slice(HALF * h, HALF * h + HALF)
                        j = 2 * g + h + 1
                        act.wait_ge(rows_in[h], 16 * HALF * (g + 1))
                        copy_indices(nc, mem, index, h, t).then_inc(index_in, 1)
                        gate, core = logits[:, b, 0:D], logits[:, b, D:2 * D]
                        act.wait_ge(logits_made, j)
                        nc.scalar.activation(gate, gate, ACT.Exp, scale=-1.0).then_inc(gate_exp, 1)
                        act.wait_ge(capped, j)
                        nc.scalar.activation(soft[:, b, :], soft[:, b, :], ACT.Exp).then_inc(exp_made, 1)
                        act.wait_ge(gate_exp, j)
                        nc.scalar.activation(gate, gate, ACT.Identity, bias=1.0).then_inc(gate_one, 1)
                        act.wait_ge(exp_made, j)
                        nc.scalar.activation(soft[:, b, :], soft[:, b, :], ACT.Ln, bias=1.0).then_inc(log_made, 1)

            @block.vector
            def _(dve):
                nc.vector.memset(mem.acc[:, :, 0:D], 0.0).then_inc(added, 1)
                dve.sem_inc(rows_free, 2)
                n = group_count(dve, mem)
                with dve.Fori(0, n) as g:
                    w, t = step_registers(dve, mem, "s3_dve", g, True, True)
                    for h in range(2):
                        dve.wait_ge(onehots_free, 2 * g + h + 1)
                        build_onehots(nc, mem, into, h, w, t).then_inc(onehots, 1)
                    for h in range(2):
                        b = slice(HALF * h, HALF * h + HALF)
                        j = 2 * g + h + 1
                        dve.wait_ge(rows_in[h], 16 * HALF * (g + 1))
                        dve.wait_ge(products, j)
                        for k in range(2):
                            c = slice(HALF * h + 2 * k, HALF * h + 2 * k + 2)
                            last = nc.vector.tensor_tensor(logits[:, c, :], rows[:, c, :], logits_ps[h][k][:], ALU.add)
                        last.then_inc(logits_made, 1)
                        dve.wait_ge(logits_made, j)
                        dve.sem_inc(rows_free, 1)
                        nc.vector.tensor_scalar(soft[:, b, :], logits[:, b, D:2 * D], SOFT_TOP, None,
                                                ALU.min).then_inc(capped, 1)
                    for h in range(2):
                        b = slice(HALF * h, HALF * h + HALF)
                        j = 2 * g + h + 1
                        gate, core = logits[:, b, 0:D], logits[:, b, D:2 * D]
                        dve.wait_ge(gate_one, j)
                        nc.vector.reciprocal(gate, gate).then_inc(gate_made, 1)
                        dve.wait_ge(log_made, j)
                        nc.vector.tensor_tensor(core, core, soft[:, b, :], ALU.max).then_inc(core_made, 1)
                        dve.wait_ge(gate_made, j)
                        dve.wait_ge(core_made, j)
                        nc.vector.tensor_tensor(soft[:, b, :], core, gate, ALU.mult).then_inc(messages, 1)
                    for h in range(2):
                        dve.wait_ge(summed, 2 * g + h + 1)
                        for i in range(HALF):
                            u = HALF * h + i
                            dve.wait_ge(added, STEPS * g + u + 1)
                            acc = window(mem.acc[:, :, 0:D], w[u])
                            nc.vector.tensor_tensor(acc, acc, sums_ps[h][:, i, :], ALU.add).then_inc(added, 1)

            @block.tensor
            def _(pe):
                pe.sem_inc(onehots_free, 2)
                pe.sem_inc(edge_free, 2)
                n = group_count(pe, mem)
                with pe.Fori(0, n) as g:
                    w, _ = step_registers(pe, mem, "s3_pe", g, True, False)
                    for h in range(2):
                        pe.wait_ge(onehots, 2 * g + h + 1)
                        for i in range(HALF):
                            last = nc.tensor.transpose(into_t_ps[h][:, i, :], into[:, HALF * h + i, :], mem.ident[:])
                        last.then_inc(turned, 1)
                    for h in range(2):
                        pe.wait_ge(edge_in[h], 16 * HALF * (g + 1))
                        pe.wait_ge(turned_copied, 2 * g + h + 1)
                        for i in range(HALF):
                            u = HALF * h + i
                            pre = logits_ps[h][i // 2][:, i % 2, :]
                            nc.tensor.matmul(pre, edge[:, u, :], mem.w3[:, 2, :], start=True, stop=False)
                            last = nc.tensor.matmul(pre, into_t[:, u, :], window(mem.nodes, w[u]),
                                                    start=False, stop=True)
                        last.then_inc(products, 1)
                        pe.wait_ge(products, 2 * g + h + 1)
                        pe.sem_inc(edge_free, 1)
                    for h in range(2):
                        pe.wait_ge(messages, 2 * g + h + 1)
                        pe.wait_ge(added, STEPS * g + 1)
                        for i in range(HALF):
                            u = HALF * h + i
                            last = nc.tensor.matmul(sums_ps[h][:, i, :], into[:, u, :], soft[:, u, :],
                                                    start=True, stop=True)
                        last.then_inc(summed, 1)
                        pe.wait_ge(summed, 2 * g + h + 1)
                        pe.sem_inc(onehots_free, 1)
                pe.wait_ge(summed, 2 * n)


def layer0(nc, mem, a):
    def scale_bias(dve):
        nc.vector.tensor_scalar(mem.b0[:], mem.b0[:], mem.agg[:], None, ALU.mult).then_inc(scaled, 1)
        dve.wait_ge(scaled, 1)

    def message(dve, w, s, sums):
        return nc.vector.scalar_tensor_tensor(mem.nodes[:, bass.ds(w, 1), 0:D].rearrange("p a b -> p (a b)"), sums[:],
                                              mem.agg[:], mem.b0[:], ALU.mult, ALU.add)

    with nc.semaphore("bias_scaled") as scaled:
        phase_project(nc, mem, "p0", [mem.x], [mem.w0[:]], D, message, scale_bias)
    phase_scatter(nc, mem, a["src_rows"])

    places = [mem.acc[:, :, 0:D], mem.acc[:, :, D:2 * D],
              mem.nodes[:, 0:WINDOWS, 0:D], mem.nodes[:, 0:WINDOWS, D:2 * D]]
    with nc.semaphore("partials_in") as arrived, nc.Block() as block:
        @block.sync
        def _(sp):
            for place, table in zip(places, mem.partial):
                sp.dma_start(place, by_window(table[0:NODES_PAD, :])).then_inc(arrived, 16)
            sp.wait_ge(arrived, 16 * TABLES)

    def add_partials(dve):
        for n, place in enumerate(places):
            nc.vector.tensor_tensor(mem.x, mem.x, place, ALU.add).then_inc(partials_added, 1)
            dve.wait_ge(partials_added, n + 1)

    with nc.semaphore("partials_added") as partials_added:
        phase_norm(nc, mem, "n0", add_partials, (mem.x_rows, True))


def layer1(nc, mem):
    phase_attend(nc, mem)
    with ExitStack() as ctx:
        inverse = ctx.enter_context(nc.sbuf_tensor("l1_inverse", [P, WINDOWS, 2], F32))
        (link,) = sems(nc, ctx, "l1_link")
        shape = [P, WINDOWS, D]

        def normalise(dve):
            nc.vector.tensor_scalar(mem.acc_small[:], mem.acc_small[:], 1e-30, None, ALU.max).then_inc(link, 1)
            nc.vector.tensor_tensor(mem.b1[:, 0, :], mem.b1[:, 0, :], mem.b1[:, 1, :], ALU.add).then_inc(link, 1)
            dve.wait_ge(link, 2)
            nc.vector.reciprocal(inverse[:], mem.acc_small[:]).then_inc(link, 1)
            nc.vector.tensor_tensor(mem.b1[:, 0, :], mem.b1[:, 0, :], mem.b1[:, 2, :], ALU.add).then_inc(link, 1)
            dve.wait_ge(link, 4)
            for j in range(2):
                part = mem.acc[:, :, j * D:j * D + D]
                nc.vector.tensor_tensor(part, part, inverse[:, :, j].unsqueeze(2).broadcast_to(shape),
                                        ALU.mult).then_inc(link, 1)
            dve.wait_ge(link, 6)

        def add_window(dve, w, s, sums):
            x = window(mem.x, w)
            return nc.vector.tensor_tensor(x, x, sums[:], ALU.add)

        def add_bias(dve):
            nc.vector.tensor_tensor(mem.x, mem.x, mem.b1[:, 0, :].unsqueeze(1).broadcast_to(shape),
                                    ALU.add).then_inc(link, 1)
            dve.wait_ge(link, 7)

        phase_project(nc, mem, "p1", [mem.acc[:, :, 0:D], mem.acc[:, :, D:2 * D], mem.x],
                      [mem.w1[:, j, :] for j in range(3)], D, add_window, normalise)
        phase_norm(nc, mem, "n1", add_bias, (mem.x_rows, True))


def layer2(nc, mem):
    phase_mean(nc, mem)
    with ExitStack() as ctx:
        def sb(name, shape):
            return ctx.enter_context(nc.sbuf_tensor("l2_" + name, shape, F32))

        inverse = sb("inverse", [P, WINDOWS])
        real = sb("real", [P, WINDOWS])
        square = sb("square", [P, WINDOWS])
        total = sb("total", [P, 2])
        over_all = sb("over_all", [P, 2])
        norm = sb("norm", [P, 2])
        link, tanh_made, squared, total_made, reduced, root_made = sems(
            nc, ctx, *("l2_" + n for n in ("link", "tanh_made", "squared", "total_made", "reduced", "root_made")))
        shape = [P, WINDOWS, D]

        def divide(dve):
            nc.vector.tensor_scalar(mem.acc_small[:], mem.acc_small[:], 1.0, None, ALU.max).then_inc(link, 1)
            dve.wait_ge(link, 1)
            nc.vector.reciprocal(inverse[:], mem.acc_small[:, :, 0]).then_inc(link, 1)
            dve.wait_ge(link, 2)
            nc.vector.tensor_tensor(mem.acc[:, :, 0:D], mem.acc[:, :, 0:D],
                                    inverse[:].unsqueeze(2).broadcast_to(shape), ALU.mult).then_inc(link, 1)
            dve.wait_ge(link, 3)

        def with_bias(dve, w, s, sums):
            return nc.vector.tensor_tensor(window(mem.nodes[:, :, 0:D], w), sums[:], mem.b2[:], ALU.add)

        phase_project(nc, mem, "p2", [mem.x, mem.acc[:, :, 0:D], mem.x],
                      [mem.w2[:, j, :] for j in range(3)], D, with_bias, divide)

        tanhs, squares = mem.nodes[:, 0:WINDOWS, 0:D], mem.acc[:, :, 0:D]
        with nc.Block() as block:
            @block.scalar
            def _(act):
                nc.scalar.activation(tanhs, tanhs, ACT.Tanh).then_inc(tanh_made, 1)
                act.wait_ge(tanh_made, 1)
                nc.scalar.activation(squares, tanhs, ACT.Square).then_inc(squared, 1)
                act.wait_ge(reduced, 1)
                nc.scalar.activation(norm[:], over_all[:], ACT.Sqrt).then_inc(root_made, 1)

            @block.vector
            def _(dve):
                nc.vector.tensor_scalar(real[:], mem.window_base[:], mem.lane[:], float(NODES), ALU.add, ALU.is_lt)
                dve.wait_ge(squared, 1)
                nc.vector.tensor_reduce(square[:], squares, AX.X, ALU.add).then_inc(link, 1)
                dve.wait_ge(link, 4)
                nc.vector.tensor_tensor(square[:], square[:], real[:], ALU.mult).then_inc(link, 1)
                dve.wait_ge(link, 5)
                for k in range(2):
                    last = nc.vector.tensor_reduce(total[:, k:k + 1], square[:], AX.X, ALU.add)
                last.then_inc(total_made, 1)
                dve.wait_ge(root_made, 1)
                nc.vector.reciprocal(total[:], norm[:]).then_inc(link, 1)
                dve.wait_ge(link, 6)

            @block.gpsimd
            def _(pool):
                pool.wait_ge(total_made, 1)
                pool.partition_all_reduce(over_all[:], total[:], P, REDUCE_ADD).then_inc(reduced, 1)

        def add_scaled(dve):
            nc.vector.scalar_tensor_tensor(mem.x, tanhs, total[:, 0:1], mem.x, ALU.mult, ALU.add).then_inc(link, 1)
            dve.wait_ge(link, 7)

        phase_norm(nc, mem, "n2", add_scaled, (mem.x_rows, True))


def layer3(nc, mem, a, out):
    with ExitStack() as ctx:
        link, halves, stored = sems(nc, ctx, "l3_link", "l3_halves", "l3_stored")

        def split(dve, w, s, sums):
            nc.vector.tensor_tensor(window(mem.nodes, w), sums[:, 0:2 * D], mem.b3[:], ALU.add)
            return nc.vector.tensor_copy(window(mem.acc, w), sums[:, 2 * D:4 * D])

        phase_project(nc, mem, "p3", [mem.x], [mem.w3[:, 0:2, :].rearrange("p a b -> p (a b)")], 4 * D, split)
        with nc.Block() as block:
            @block.sync
            def _(sp):
                sp.dma_start(by_window(mem.b_rows), mem.acc[:]).then_inc(stored, 16)
                sp.wait_ge(stored, 16)

        phase_gate(nc, mem, a["edge_attr"])

        def add_acc(dve):
            nc.vector.scalar_tensor_tensor(mem.x, mem.x, 2.0, mem.acc[:, :, 0:D], ALU.mult, ALU.add).then_inc(link, 1)
            dve.wait_ge(link, 1)

        phase_norm(nc, mem, "n3", add_acc, (out, False))




def build(nc, a, out):
    with ExitStack() as ctx:
        mem = Memory(nc, ctx)
        phase_setup(nc, mem, a)
        layer0(nc, mem, a)
        layer1(nc, mem)
        layer2(nc, mem)
        layer3(nc, mem, a, out)


def kernel(**inputs):
    import numpy as np
    import concourse.bacc as bacc
    from concourse.bass_utils import run_bass_kernel_spmd

    def edges(name, fill, rows):
        a = np.asarray(inputs[name])
        return np.concatenate([a, np.full(rows * P - EDGES, fill, a.dtype)]).reshape(rows, P)

    def nodes(name):
        a = np.asarray(inputs[name])
        return np.concatenate([a, np.zeros((NODES_PAD - NODES,) + a.shape[1:], a.dtype)])

    def row(name):
        return np.asarray(inputs[name]).reshape(1, -1)

    edge_attr = np.asarray(inputs["edge_attr_128"])
    parts = (3, D, D)
    gate_core = [np.asarray(inputs["L3_gnn_" + n]).reshape(parts) for n in ("W_f", "W_s")]
    arrays = {
        "x": nodes("x"),
        "src_cols": edges("src", 0, TILES_PAD).T,
        "src_rows": edges("src", 0, TILES_PAD),
        "dst_cols": edges("dst", NOWHERE, TILES_PAD).T,
        "dst_tiles": edges("dst", NOWHERE, TILE_ROWS * P).reshape(TILE_ROWS, P, P).transpose(1, 0, 2),
        "edge_attr": np.concatenate([edge_attr, np.zeros((TILES_PAD * P - EDGES, D), edge_attr.dtype)]).T,
        "node_vec_cols": nodes("node_vec").reshape(WINDOWS, P).T,
        "node_vec_rows": nodes("node_vec").reshape(NODES_PAD, 1),
        "L0_W": np.asarray(inputs["L0_gnn_W"]).T,
        "L0_b": row("L0_gnn_b"),
        "L0_gnn_agg_weight": row("L0_gnn_agg_weight"),
        "L1_W_homo": np.asarray(inputs["L1_gnn_W_homo"]),
        "L1_W_hete": np.asarray(inputs["L1_gnn_W_hete"]),
        "L1_W_self": np.asarray(inputs["L1_gnn_W_self"]),
        "L1_b_homo": row("L1_gnn_b_homo"),
        "L1_b_hete": row("L1_gnn_b_hete"),
        "L1_b_self": row("L1_gnn_b_self"),
        "L2_W": np.asarray(inputs["L2_gnn_W"]).T.reshape(3, D, D).transpose(1, 0, 2),
        "L2_b": row("L2_gnn_b"),
        "L3_W": np.stack(gate_core, 2).reshape(3, D, 2 * D).transpose(1, 0, 2),
        "L3_b": np.concatenate([row("L3_gnn_b_f"), row("L3_gnn_b_s")], 1),
    }
    arrays = {n: np.ascontiguousarray(a) for n, a in arrays.items()}
    nc = bacc.Bacc("TRN2", target_bir_lowering=False, num_devices=1)
    a = {n: nc.dram_tensor(n, v.shape, mybir.dt.from_np(v.dtype), kind="ExternalInput").ap()
         for n, v in arrays.items()}
    out = nc.dram_tensor("out", (NODES, D), F32, kind="ExternalOutput").ap()
    build(nc, a, out)
    result = run_bass_kernel_spmd(nc, [arrays], core_ids=[0])
    return result.results[0]["out"]
```

```python
import concourse.bass as bass
from concourse import mybir
from contextlib import ExitStack

F32 = mybir.dt.float32
BF16 = mybir.dt.bfloat16
I32 = mybir.dt.int32
ALU = mybir.AluOpType
ACT = mybir.ActivationFunctionType
AX = mybir.AxisListType
REDUCE_MAX = bass.bass_isa.ReduceOp.max
REDUCE_ADD = bass.bass_isa.ReduceOp.add

P = 128
D = 128
NODES = 6250
EDGES = 106250
WINDOWS = 50
NODES_PAD = WINDOWS * P
NOWHERE = NODES_PAD
TILES = -(-EDGES // P)
EMPTY_TILE = TILES
TILES_PAD = TILES + 1
TILE_ROWS = -(-TILES // P)
HALF = 4
STEPS = 2 * HALF
GROUPS_PER_PARTITION = 41
GROUPS_MAX = P * GROUPS_PER_PARTITION
assert GROUPS_MAX * STEPS >= TILES * WINDOWS + 2 * STEPS
ROW_PARTS = 4
STEP_COLUMNS = (GROUPS_PER_PARTITION + 1) * STEPS
TABLES = 4
SCATTER_ROWS = NODES_PAD + P
TILE_CODE = 64
FAR = 1000.0
EPS = 1e-5
SLOPE = 0.2
SOFT_RANGE = 60.0
LOWEST = -3.0e38
EXP_LN_SET = 6


class Memory:

    def __init__(self, nc, ctx):
        def sb(name, shape, dtype=F32):
            return ctx.enter_context(nc.sbuf_tensor(name, shape, dtype))

        self.nc = nc
        self.turn = ctx.enter_context(nc.semaphore("turn"))
        self.projection = sems(nc, ctx, *("project_" + s for s in (
            "transposed", "copied", "summed", "sums_free", "prepared", "first_staged", "others_staged",
            "staged_free")))
        self.projections = 0
        self.x_one = sb("x_one", [P, WINDOWS, D + 2])
        self.x = self.x_one[:, :, 0:D]
        self.v = sb("v", [P, WINDOWS])
        self.acc = sb("acc", [P, WINDOWS, 2 * D + 2])
        self.nodes = sb("nodes", [P, 51, 2 * D + 2])
        self.src_i = sb("src_i", [P, TILES_PAD], I32)
        self.src_f = sb("src_f", [P, TILES_PAD])
        self.dst_f = sb("dst_f", [P, TILES_PAD])
        self.window_base = sb("window_base", [P, WINDOWS])
        self.column = sb("column", [P, P])
        self.lane = sb("lane", [P, 1])
        self.ident = sb("ident", [P, P])
        self.shift = sb("shift", [P, WINDOWS, 2])
        self.v_top = sb("v_top", [P, 2])
        self.groups = sb("groups", [P, 1], I32)
        self.passes = sb("passes", [P, 4], I32)
        self.agg = sb("agg", [P, 1])
        self.xt = sb("xt", [P, 2, 3, P])
        self.w0 = sb("w0", [P, D])
        self.w1 = sb("w1", [P, 3, D])
        self.w2 = sb("w2", [P, 3, D])
        self.w3 = sb("w3", [P, 3, 2 * D])
        self.b0 = sb("b0", [P, D])
        self.b1 = sb("b1", [P, 3, D])
        self.b2 = sb("b2", [P, D])
        self.b3 = sb("b3", [P, 2 * D])
        self.steps = nc.dram_tensor("steps", [GROUPS_MAX, ROW_PARTS * STEPS], I32).ap()
        self.partial = [nc.dram_tensor(f"partial{i}", [SCATTER_ROWS, D], F32).ap() for i in range(TABLES)]
        self.x_rows = nc.dram_tensor("x_rows", [NODES_PAD, D + 2], F32).ap()
        self.weighted_rows = nc.dram_tensor("weighted_rows", [NODES_PAD, 2 * D + 2], F32).ap()
        self.b_rows = nc.dram_tensor("b_rows", [NODES_PAD, 2 * D], F32).ap()


def sems(nc, ctx, *names):
    return [ctx.enter_context(nc.semaphore(n)) for n in names]


def by_window(rows):
    return rows.rearrange("(w p) d -> p w d", p=P)


def step_registers(eng, mem, name, group, windows=False, tiles=False, before=False):
    limits = [WINDOWS - 1] * STEPS + [TILES_PAD - 1] * STEPS + [WINDOWS - 1] * STEPS
    asked = [k for k, on in enumerate((windows, tiles, before)) if on]
    first, end = asked[0] * STEPS, (asked[-1] + 1) * STEPS
    regs = [eng.alloc_register(f"{name}{u}") for u in range(first, end)]
    if not isinstance(group, int):
        group = mem.nc.s_assert_within(group, 0, GROUPS_MAX - 1, skip_runtime_bounds_check_because=(
            "a group is at most the one after the last, and group_count() is GROUPS_MAX - 2 at most"))
    eng.load(regs, mem.steps[bass.ds(group, 1), first:end])
    values = [eng.snap(r, donate=True, min_val=0, max_val=limits[u]) for u, r in zip(range(first, end), regs)]
    return [values[k * STEPS - first:(k + 1) * STEPS - first] for k in range(asked[0], asked[-1] + 1)]


def group_count(eng, mem):
    return eng.value_load(mem.groups[0:1, 0:1], min_val=1, max_val=GROUPS_MAX - 2)


def all_groups(eng, mem):
    return group_count(eng, mem), 0


def groups_if_wide(eng, mem):
    return [eng.value_load(mem.passes[0:1, k:k + 1], min_val=k == 0, max_val=GROUPS_MAX - 2) for k in range(2)]


def groups_unless_wide(eng, mem):
    return [eng.value_load(mem.passes[0:1, k:k + 1], min_val=k == 2, max_val=GROUPS_MAX - 2) for k in range(2, 4)]


def window(ap, w):
    return ap[:, bass.ds(w, 1), :].rearrange("p a b -> p (a b)")


def phase_setup(nc, mem, a):
    with ExitStack() as ctx:
        def sb(name, shape, dtype=F32):
            return ctx.enter_context(nc.sbuf_tensor(name, shape, dtype))

        dst_i = sb("dst_i", [P, TILES_PAD], I32)
        lane_i = sb("lane_i", [P, 1], I32)
        column_i = sb("column_i", [P, P], I32)
        base_i = sb("base_i", [P, WINDOWS], I32)
        tile_i = sb("tile_i", [P, TILE_ROWS], I32)
        step_i = sb("step_i", [P, STEP_COLUMNS], I32)
        tile_dst = sb("tile_dst", [P, TILE_ROWS, P], I32)
        v_in = sb("v_in", [P, WINDOWS])
        tile_no = sb("tile_no", [P, TILE_ROWS])
        lowest = sb("lowest", [P, TILE_ROWS])
        highest = sb("highest", [P, TILE_ROWS])
        low_side = sb("low_side", [P, WINDOWS, TILE_ROWS])
        high_side = sb("high_side", [P, WINDOWS, TILE_ROWS])
        first_last = sb("first_last", [P, 2 * WINDOWS + 2])
        over_all = sb("over_all", [P, 2 * WINDOWS + 2])
        count = sb("count", [P, WINDOWS])
        ended = sb("ended", [P, WINDOWS])
        jump = sb("jump", [P, WINDOWS])
        ones = sb("ones", [P, WINDOWS])
        step_f = sb("step_f", [P, STEP_COLUMNS])
        code = sb("code", [P, STEP_COLUMNS])
        part = sb("part", [P, STEP_COLUMNS])
        code_i = sb("code_i", [P, STEP_COLUMNS], I32)
        decoded = sb("decoded", [P, GROUPS_PER_PARTITION, ROW_PARTS, STEPS], I32)
        small = sb("small", [P, 4])
        (indices_in, tiles_in, nodes_in, const_made, link, edges_ready, all_reduced,
         zeros_made, steps_made, stored) = sems(
            nc, ctx, "indices_in", "tiles_in", "nodes_in", "const_made", "setup_link", "edges_ready",
            "all_reduced", "zeros_made", "steps_made", "setup_stored")

        with nc.Block() as block:
            @block.sync
            def _(sp):
                sp.dma_start(tile_dst[:], a["dst_tiles"]).then_inc(tiles_in, 16)
                sp.dma_start(v_in[:], a["node_vec_cols"]).then_inc(tiles_in, 16)
                sp.dma_start(mem.src_i[:], a["src_cols"]).then_inc(indices_in, 16)
                sp.dma_start(dst_i[:], a["dst_cols"]).then_inc(indices_in, 16)
                sp.dma_start(mem.x, by_window(a["x"])).then_inc(nodes_in, 16)
                sp.dma_start(mem.agg[:], a["L0_gnn_agg_weight"].broadcast_to([P, 1])).then_inc(nodes_in, 16)
                for dst, name in ((mem.w0, "L0_W"), (mem.w2, "L2_W"), (mem.w3, "L3_W")):
                    sp.dma_start(dst[:], a[name]).then_inc(nodes_in, 16)
                for j, name in enumerate(("homo", "hete", "self")):
                    sp.dma_start(mem.w1[:, j, :], a["L1_W_" + name]).then_inc(nodes_in, 16)
                    sp.dma_start(mem.b1[:, j, :], a["L1_b_" + name].broadcast_to([P, D])).then_inc(nodes_in, 16)
                for dst, name in ((mem.b0, "L0_b"), (mem.b2, "L2_b"), (mem.b3, "L3_b")):
                    sp.dma_start(dst[:], a[name].broadcast_to(list(dst.shape))).then_inc(nodes_in, 16)
                sp.wait_ge(zeros_made, 1)
                for table in mem.partial:
                    sp.dma_start(table.rearrange("(p r) d -> p (r d)", p=P),
                                 mem.nodes[:].rearrange("p w d -> p (w d)")[:, 0:SCATTER_ROWS // P * D]
                                 ).then_inc(stored, 16)
                sp.wait_ge(steps_made, 1)
                sp.dma_start(mem.steps.rearrange("(p g) s -> p (g s)", p=P),
                             decoded[:].rearrange("p g k s -> p (g k s)")).then_inc(stored, 16)
                sp.wait_ge(nodes_in, 16 * 14)
                sp.wait_ge(stored, 16 * (TABLES + 1))

            @block.gpsimd
            def _(pool):
                pool.iota(lane_i[:], [[0, 1]], base=0, channel_multiplier=1)
                pool.iota(column_i[:], [[1, P]], base=0, channel_multiplier=0)
                pool.iota(base_i[:], [[P, WINDOWS]], base=0, channel_multiplier=0)
                pool.iota(tile_i[:], [[P, TILE_ROWS]], base=0, channel_multiplier=1)
                pool.iota(step_i[:], [[1, STEP_COLUMNS]], base=-STEPS,
                          channel_multiplier=GROUPS_PER_PARTITION * STEPS).then_inc(const_made, 1)
                pool.memset(mem.nodes[:], 0.0).then_inc(zeros_made, 1)
                pool.wait_ge(edges_ready, 1)
                pool.partition_all_reduce(over_all[:], first_last[:], P, REDUCE_MAX).then_inc(all_reduced, 1)

            @block.vector
            def _(dve):
                done = [0]

                def link_op(ins):
                    done[0] += 1
                    ins.then_inc(link, 1)
                    dve.wait_ge(link, done[0])

                dve.wait_ge(const_made, 1)
                nc.vector.tensor_copy(mem.lane[:], lane_i[:])
                nc.vector.tensor_copy(mem.column[:], column_i[:])
                nc.vector.tensor_copy(mem.window_base[:], base_i[:])
                nc.vector.tensor_copy(tile_no[:], tile_i[:])
                nc.vector.memset(ones[:], 1.0)
                nc.vector.memset(mem.x_one[:, :, D:D + 2], 1.0)
                link_op(nc.vector.tensor_copy(step_f[:], step_i[:]))
                nc.vector.tensor_scalar(mem.ident[:], mem.column[:], mem.lane[:], None, ALU.is_equal)
                dve.wait_ge(tiles_in, 32)
                nc.vector.tensor_reduce(lowest[:], tile_dst[:], AX.X, ALU.min)
                link_op(nc.vector.tensor_reduce(highest[:], tile_dst[:], AX.X, ALU.max))
                shape = [P, WINDOWS, TILE_ROWS]
                base = mem.window_base[:].unsqueeze(2).broadcast_to(shape)
                nc.vector.tensor_tensor(low_side[:], base, lowest[:].unsqueeze(1).broadcast_to(shape), ALU.subtract)
                link_op(nc.vector.tensor_tensor(high_side[:], highest[:].unsqueeze(1).broadcast_to(shape), base, ALU.subtract))
                link_op(nc.vector.tensor_scalar(high_side[:], high_side[:], 0.0, None, ALU.is_ge))
                link_op(nc.vector.scalar_tensor_tensor(low_side[:], low_side[:], float(1 - P), high_side[:],
                                                       ALU.is_ge, ALU.mult))
                tiles = tile_no[:].unsqueeze(1).broadcast_to(shape)
                link_op(nc.vector.scalar_tensor_tensor(high_side[:], tiles, 1.0, low_side[:], ALU.add, ALU.mult))
                link_op(nc.vector.tensor_scalar(tile_no[:], tile_no[:], -1.0, FAR, ALU.mult, ALU.add))
                link_op(nc.vector.tensor_tensor(low_side[:], low_side[:], tiles, ALU.mult))
                nc.vector.tensor_reduce(first_last[:, 0:WINDOWS], high_side[:], AX.X, ALU.max)
                nc.vector.tensor_reduce(first_last[:, WINDOWS:2 * WINDOWS], low_side[:], AX.X, ALU.max)
                link_op(nc.vector.tensor_scalar(count[:], v_in[:], -1.0, None, ALU.mult))
                nc.vector.tensor_reduce(first_last[:, 2 * WINDOWS:2 * WINDOWS + 1], v_in[:], AX.X, ALU.max)
                nc.vector.tensor_reduce(first_last[:, 2 * WINDOWS + 1:2 * WINDOWS + 2], count[:], AX.X,
                                        ALU.max).then_inc(edges_ready, 1)
                nc.vector.tensor_copy(mem.v[:], v_in[:])
                dve.wait_ge(indices_in, 32)
                nc.vector.tensor_copy(mem.src_f[:], mem.src_i[:])
                nc.vector.tensor_copy(mem.dst_f[:], dst_i[:])
                dve.wait_ge(all_reduced, 1)
                last1, far_first = over_all[:, 0:WINDOWS], over_all[:, WINDOWS:2 * WINDOWS]
                v_top = over_all[:, 2 * WINDOWS:2 * WINDOWS + 2]
                nc.vector.tensor_copy(mem.v_top[:], v_top)
                link_op(nc.vector.tensor_tensor(count[:], last1, far_first, ALU.add))
                link_op(nc.vector.tensor_scalar(jump[:], last1, 0.0, None, ALU.is_gt))
                link_op(nc.vector.scalar_tensor_tensor(count[:], count[:], -FAR, jump[:], ALU.add, ALU.mult))
                link_op(nc.vector.tensor_tensor_scan(ended[:], ones[:], count[:], 0.0, ALU.mult, ALU.add))
                link_op(nc.vector.tensor_tensor(count[:], count[:], ended[:], ALU.subtract))
                link_op(nc.vector.tensor_tensor(count[:], count[:], far_first, ALU.subtract))
                link_op(nc.vector.tensor_scalar(count[:], count[:], FAR, None, ALU.add))
                link_op(nc.vector.tensor_tensor(jump[:, 0:WINDOWS - 1], count[:, 1:WINDOWS], count[:, 0:WINDOWS - 1],
                                                ALU.subtract))
                link_op(nc.vector.tensor_scalar(jump[:, 0:WINDOWS - 1], jump[:, 0:WINDOWS - 1], float(TILE_CODE), 1.0,
                                                ALU.mult, ALU.add))
                link_op(nc.vector.tensor_scalar(code[:], step_f[:], count[:, 0:1], float(TILE_CODE),
                                                ALU.add, ALU.mult))
                for w in range(WINDOWS - 1):
                    link_op(nc.vector.tensor_scalar(part[:], step_f[:], ended[:, w:w + 1], jump[:, w:w + 1],
                                                    ALU.is_ge, ALU.mult))
                    link_op(nc.vector.tensor_tensor(code[:], code[:], part[:], ALU.add))
                total = ended[:, WINDOWS - 1:WINDOWS]
                link_op(nc.vector.scalar_tensor_tensor(code[:], step_f[:], total, code[:], ALU.is_lt, ALU.mult))
                link_op(nc.vector.tensor_scalar(part[:], step_f[:], total, float(TILE_CODE * EMPTY_TILE + WINDOWS - 1),
                                                ALU.is_ge, ALU.mult))
                link_op(nc.vector.tensor_tensor(code_i[:], code[:], part[:], ALU.add))
                coded = code_i[:].rearrange("p (g s) -> p g s", s=STEPS)
                now, before = coded[:, 1:GROUPS_PER_PARTITION + 1, :], coded[:, 0:GROUPS_PER_PARTITION, :]
                nc.vector.memset(decoded[:, :, 3, :], 0)
                nc.vector.tensor_scalar(decoded[:, :, 0, :], now, TILE_CODE - 1, None, ALU.bitwise_and)
                nc.vector.tensor_scalar(decoded[:, :, 2, :], before, TILE_CODE - 1, None, ALU.bitwise_and)
                nc.vector.tensor_scalar(decoded[:, :, 1, :], now, 6, None,
                                        ALU.logical_shift_right).then_inc(steps_made, 1)
                link_op(nc.vector.tensor_scalar(small[:, 0:1], total, float(STEPS - 1), float(STEPS), ALU.add, ALU.max))
                link_op(nc.vector.tensor_copy(mem.groups[:], small[:, 0:1]))
                link_op(nc.vector.tensor_scalar(mem.groups[:], mem.groups[:], 3, None, ALU.logical_shift_right))
                link_op(nc.vector.tensor_tensor(small[:, 1:2], mem.v_top[:, 0:1], mem.v_top[:, 1:2], ALU.add))
                link_op(nc.vector.tensor_scalar(small[:, 1:2], small[:, 1:2], SOFT_RANGE, None, ALU.is_le))
                link_op(nc.vector.tensor_copy(small[:, 0:1], mem.groups[:]))
                link_op(nc.vector.tensor_tensor(small[:, 1:2], small[:, 0:1], small[:, 1:2], ALU.mult))
                link_op(nc.vector.tensor_tensor(small[:, 0:1], small[:, 0:1], small[:, 1:2], ALU.subtract))
                nc.vector.tensor_scalar(mem.passes[:, 0:1], small[:, 0:1], 1.0, None, ALU.max)
                nc.vector.tensor_copy(mem.passes[:, 1:2], small[:, 1:2])
                nc.vector.tensor_scalar(mem.passes[:, 2:3], small[:, 1:2], 1.0, None, ALU.max)
                nc.vector.tensor_copy(mem.passes[:, 3:4], small[:, 0:1])
                link_op(nc.vector.scalar_tensor_tensor(small[:, 2:4], mem.v_top[:], SLOPE, mem.v_top[:],
                                                       ALU.mult, ALU.max))
                nc.vector.tensor_copy(mem.shift[:], small[:, 2:4].unsqueeze(1).broadcast_to([P, WINDOWS, 2]))


def phase_project(nc, mem, name, sources, products, width, finish, prepare=None):
    with ExitStack() as ctx:
        def ps(tag, shape):
            return [ctx.enter_context(nc.psum_tensor(f"{name}_{tag}{s}", shape, F32)) for s in range(2)]

        turned, sums = ps("turned", [P, len(sources), P]), ps("sums", [P, width])
        staged = ctx.enter_context(nc.sbuf_tensor(f"{name}_staged", [P, 2, len(sources), P], F32))
        transposed, copied, summed, sums_free, prepared, first_staged, others_staged, staged_free = mem.projection
        before = WINDOWS * mem.projections
        mem.projections += 1
        passes = WINDOWS // 2
        with nc.Block() as block:
            @block.gpsimd
            def _(pool):
                pool.wait_ge(prepared, mem.projections)
                with pool.Fori(0, passes) as i:
                    for s in range(2):
                        pool.wait_ge(staged_free, before + 2 * i + s + 1)
                        pool.sem_inc(mem.turn, 1)
                        pool.tensor_copy(staged[:, s, 0:1, :], sources[0][:, bass.ds(2 * i + s, 1), :]
                                         ).then_inc(first_staged, 1)

            @block.tensor
            def _(pe):
                if before == 0:
                    pe.sem_inc(staged_free, 2)
                with pe.Fori(0, passes) as i:
                    for s in range(2):
                        pe.wait_ge(first_staged, before + 2 * i + s + 1)
                        pe.wait_ge(others_staged, before + 2 * i + s + 1)
                        for j in range(len(sources)):
                            last = nc.tensor.transpose(turned[s][:, j, :], staged[:, s, j, :], mem.ident[:])
                        last.then_inc(transposed, 1)
                    for s in range(2):
                        pe.wait_ge(copied, before + 2 * i + s + 1)
                        pe.wait_ge(sums_free, before + 2 * i + s + 1)
                        for k, (j, weight) in enumerate(products):
                            last = nc.tensor.matmul(sums[s][:], mem.xt[:, s, j, :], weight,
                                                    start=(k == 0), stop=(k == len(products) - 1))
                        last.then_inc(summed, 1)

            @block.scalar
            def _(act):
                with act.Fori(0, passes) as i:
                    for s in range(2):
                        act.wait_ge(transposed, before + 2 * i + s + 1)
                        act.sem_inc(staged_free, 1)
                        nc.scalar.activation(mem.xt[:, s, 0:len(sources), :], turned[s][:],
                                             ACT.Copy).then_inc(copied, 1)

            @block.vector
            def _(dve):
                def stage(w, s):
                    if len(sources) == 1:
                        dve.sem_inc(others_staged, 1)
                        return
                    dve.wait_ge(staged_free, before + w + 1)
                    for j, source in enumerate(sources[1:], 1):
                        last = nc.vector.tensor_copy(staged[:, s, j:j + 1, :], source[:, bass.ds(w, 1), :])
                    last.then_inc(others_staged, 1)

                def finish_pass(i):
                    for s in range(2):
                        dve.wait_ge(summed, before + 2 * i + s + 1)
                        finish(dve, 2 * i + s, sums[s]).then_inc(sums_free, 1)

                if prepare:
                    prepare(dve)
                dve.sem_inc(prepared, 1)
                if before == 0:
                    dve.sem_inc(sums_free, 2)
                for s in range(2):
                    stage(s, s)
                with dve.Fori(0, passes - 1) as i:
                    for s in range(2):
                        stage(2 * i + 2 + s, s)
                    finish_pass(i)
                finish_pass(passes - 1)


CHUNK = 10


def phase_norm(nc, mem, name, before, store):
    chunks = [slice(c, c + CHUNK) for c in range(0, WINDOWS, CHUNK)]
    with ExitStack() as ctx:
        total = ctx.enter_context(nc.sbuf_tensor(f"{name}_total", [P, WINDOWS], F32))
        mean = ctx.enter_context(nc.sbuf_tensor(f"{name}_mean", [P, WINDOWS], F32))
        square = ctx.enter_context(nc.sbuf_tensor(f"{name}_square", [P, WINDOWS], F32))
        var = ctx.enter_context(nc.sbuf_tensor(f"{name}_var", [P, WINDOWS], F32))
        sigma = ctx.enter_context(nc.sbuf_tensor(f"{name}_sigma", [P, WINDOWS], F32))
        scale = ctx.enter_context(nc.sbuf_tensor(f"{name}_scale", [P, WINDOWS], F32))
        squares = mem.acc[:, :, 0:D]
        step, centred, squared, var_made, sigma_made, normed, stored = sems(
            nc, ctx, *(f"{name}_{s}" for s in (
                "step", "centred", "squared", "var_made", "sigma_made", "normed", "stored")))
        shape = [P, CHUNK, D]
        with nc.Block() as block:
            @block.vector
            def _(dve):
                before(dve)
                for n, c in enumerate(chunks):
                    nc.vector.tensor_reduce(total[:, c], mem.x[:, c, :], AX.X, ALU.add).then_inc(step, 1)
                    dve.wait_ge(step, 2 * n + 1)
                    nc.vector.tensor_scalar(mean[:, c], total[:, c], 1.0 / D, None, ALU.mult).then_inc(step, 1)
                    dve.wait_ge(step, 2 * n + 2)
                    nc.vector.tensor_tensor(mem.x[:, c, :], mem.x[:, c, :],
                                            mean[:, c].unsqueeze(2).broadcast_to(shape),
                                            ALU.subtract).then_inc(centred, 1)
                for n, c in enumerate(chunks):
                    dve.wait_ge(squared, n + 1)
                    last = nc.vector.tensor_reduce(square[:, c], squares[:, c, :], AX.X, ALU.add)
                base = 2 * len(chunks)
                last.then_inc(step, 1)
                dve.wait_ge(step, base + 1)
                nc.vector.tensor_scalar(var[:], square[:], 1.0 / D, EPS, ALU.mult, ALU.add).then_inc(var_made, 1)
                dve.wait_ge(sigma_made, 1)
                nc.vector.reciprocal(scale[:], sigma[:]).then_inc(step, 1)
                dve.wait_ge(step, base + 2)
                for c in chunks:
                    nc.vector.tensor_tensor(mem.x[:, c, :], mem.x[:, c, :],
                                            scale[:, c].unsqueeze(2).broadcast_to(shape),
                                            ALU.mult).then_inc(normed, 1)

            @block.scalar
            def _(act):
                for n, c in enumerate(chunks):
                    act.wait_ge(centred, n + 1)
                    nc.scalar.activation(squares[:, c, :], mem.x[:, c, :], ACT.Square).then_inc(squared, 1)
                act.wait_ge(var_made, 1)
                nc.scalar.activation(sigma[:], var[:], ACT.Sqrt).then_inc(sigma_made, 1)

            @block.sync
            def _(sp):
                if not store:
                    return
                sent = 0
                rows, with_ones = store
                for n, c in enumerate(chunks):
                    sp.wait_ge(normed, n + 1)
                    first, end = c.start * P, min(c.stop * P, rows.shape[0])
                    whole = (end - first) // P
                    source = mem.x_one if with_ones else mem.x
                    sp.dma_start(by_window(rows[first:first + whole * P, :]),
                                 source[:, c.start:c.start + whole, :]).then_inc(stored, 16)
                    sent += 1
                    if first + whole * P < end:
                        rest = end - first - whole * P
                        sp.dma_start(rows[first + whole * P:end, :],
                                     source[0:rest, c.start + whole, :]).then_inc(stored, 16)
                        sent += 1
                        break
                sp.wait_ge(stored, 16 * sent)


def phase_scatter(nc, mem, src_rows):
    with ExitStack() as ctx:
        def sb(name, shape, dtype=F32):
            return ctx.enter_context(nc.sbuf_tensor(name, shape, dtype))

        def pair(name):
            return [ctx.enter_context(nc.psum_tensor(f"{name}{h}", [P, HALF, P], F32)) for h in range(2)]

        not_later = sb("s0_not_later", [P, P])
        to_trash = sb("s0_to_trash", [P, TILES_PAD])
        sources = sb("s0_sources", [P, STEPS, P], I32)
        into = sb("s0_into", [P, STEPS, P], BF16)
        same = sb("s0_same", [P, STEPS, P], BF16)
        count = sb("s0_count", [P, STEPS])
        repeat = sb("s0_repeat", [P, STEPS])
        rows = sb("s0_rows", [P, STEPS], I32)
        primer = sb("s0_primer", [1, 3 * TABLES, P], I32)
        mix = sb("s0_mix", [P, STEPS, P])
        tile = sb("s0_tile", [P, STEPS, D])
        mix_ps, tile_ps = pair("s0_mix_ps"), pair("s0_tile_ps")
        (set_up, sources_free, onehots_free, onehots, repeat_made, rows_made, mixed, mix_copied,
         tile_summed, tile_copied) = sems(nc, ctx, *("s0_" + n for n in (
             "set_up", "sources_free", "onehots_free", "onehots", "repeat_made", "rows_made",
             "mixed", "mix_copied", "tile_summed", "tile_copied")))
        sources_in = sems(nc, ctx, "s0_sources_in0", "s0_sources_in1")
        added = sems(nc, ctx, *(f"s0_added{i}" for i in range(TABLES)))
        with nc.Block() as block:
            @block.sync
            def _(sp):
                n = group_count(sp, mem)
                with sp.Fori(0, n) as g:
                    (t,) = step_registers(sp, mem, "s0_sp", g, tiles=True)
                    for h in range(2):
                        sp.wait_ge(sources_free, 2 * g + h + 1)
                        for i in range(HALF):
                            u = HALF * h + i
                            sp.dma_start(sources[:, u, :], src_rows[bass.ds(t[u], 1), :].broadcast_to([P, P])
                                         ).then_inc(sources_in[h], 16)

            @block.vector
            def _(dve):
                nc.vector.memset(mix[:], 0.0).then_inc(set_up, 1)
                nc.vector.tensor_scalar(not_later[:], mem.column[:], mem.lane[:], None, ALU.is_le)
                nc.vector.tensor_scalar(to_trash[:], mem.src_f[:], -1.0, float(NODES_PAD),
                                        ALU.mult, ALU.add).then_inc(set_up, 1)
                dve.wait_ge(set_up, 2)
                nc.vector.tensor_scalar(to_trash[:], to_trash[:], mem.lane[:], None, ALU.add).then_inc(set_up, 1)
                dve.wait_ge(set_up, 3)
                dve.sem_inc(sources_free, 2)
                n = group_count(dve, mem)
                with dve.Fori(0, n) as g:
                    w, t = step_registers(dve, mem, "s0_dve", g, windows=True, tiles=True)
                    for h in range(2):
                        dve.wait_ge(onehots_free, 2 * g + h + 1)
                        for i in range(HALF):
                            u = HALF * h + i
                            nc.vector.tensor_scalar(into[:, u, :], mem.column[:], mem.window_base[:, bass.ds(w[u], 1)],
                                                    mem.dst_f[:, bass.ds(t[u], 1)], ALU.add, ALU.is_equal)
                        dve.wait_ge(sources_in[h], 16 * HALF * (g + 1))
                        for i in range(HALF):
                            u = HALF * h + i
                            last = nc.vector.scalar_tensor_tensor(same[:, u, :], sources[:, u, :],
                                                                  mem.src_f[:, bass.ds(t[u], 1)], not_later[:],
                                                                  ALU.is_equal, ALU.mult, accum_out=count[:, u:u + 1])
                        last.then_inc(onehots, 1)
                        dve.wait_ge(onehots, 2 * g + h + 1)
                        dve.sem_inc(sources_free, 1)
                        b = slice(HALF * h, HALF * h + HALF)
                        dve.wait_ge(rows_made, 2 * g + h + 1)
                        nc.vector.tensor_scalar(repeat[:, b], count[:, b], 1.0, None, ALU.is_gt).then_inc(repeat_made, 1)

            @block.tensor
            def _(pe):
                pe.sem_inc(onehots_free, 2)
                pe.wait_ge(set_up, 3)

                def sum_tiles(h, windows):
                    for i in range(HALF):
                        u = HALF * h + i
                        last = nc.tensor.matmul(tile_ps[h][:, i, :], mix[:, u, :],
                                                window(mem.nodes[:, :, 0:D], windows[u]), start=True, stop=True)
                    last.then_inc(tile_summed, 1)

                n = group_count(pe, mem)
                with pe.Fori(0, n) as g:
                    w, _, w_before = step_registers(pe, mem, "s0_pe", g, windows=True, before=True)
                    for h in range(2):
                        pe.wait_ge(onehots, 2 * g + h + 1)
                        for i in range(HALF):
                            last = nc.tensor.matmul(mix_ps[h][:, i, :], into[:, HALF * h + i, :],
                                                    same[:, HALF * h + i, :], start=True, stop=True)
                        last.then_inc(mixed, 1)
                        pe.wait_ge(mix_copied, 2 * g + h + 1)
                        sum_tiles(1 - h, w if h else w_before)
                _, _, w_before = step_registers(pe, mem, "s0_pe_last", n, windows=True, before=True)
                pe.wait_ge(mix_copied, 2 * n + 1)
                sum_tiles(1, w_before)

            @block.scalar
            def _(act):
                act.sem_inc(mix_copied, 1)

                def copy_tiles(j, h):
                    act.wait_ge(tile_summed, j + 1)
                    for i in range(TABLES):
                        act.wait_ge(added[i], 16 * j + 16)
                    nc.scalar.activation(tile[:, HALF * h:HALF * h + HALF, :], tile_ps[h][:],
                                         ACT.Copy).then_inc(tile_copied, 1)

                act.sem_inc(rows_made, 2)
                act.wait_ge(set_up, 3)
                n = group_count(act, mem)
                with act.Fori(0, n) as g:
                    (t,) = step_registers(act, mem, "s0_act", g, tiles=True)
                    for h in range(2):
                        act.wait_ge(mixed, 2 * g + h + 1)
                        act.wait_ge(tile_summed, 2 * g + h + 1)
                        act.sem_inc(onehots_free, 1)
                        nc.scalar.activation(mix[:, HALF * h:HALF * h + HALF, :], mix_ps[h][:],
                                             ACT.Copy).then_inc(mix_copied, 1)
                        copy_tiles(2 * g + h, 1 - h)
                        act.wait_ge(repeat_made, 2 * g + h + 1)
                        for i in range(TABLES):
                            act.wait_ge(added[i], 16 * (2 * g + h) + 32)
                        for i in range(HALF):
                            u = HALF * h + i
                            last = nc.scalar.activation(rows[:, u:u + 1], repeat[:, u:u + 1], ACT.Identity,
                                                        bias=mem.src_f[:, bass.ds(t[u], 1)],
                                                        scale=to_trash[:, bass.ds(t[u], 1)])
                        last.then_inc(rows_made, 1)
                copy_tiles(2 * n, 1)

            @block.gpsimd
            def _(pool):
                for k in range(3):
                    for i in range(TABLES):
                        pool.dma_start(primer[0:1, 3 * i + k, :], src_rows[0:1, :]).then_inc(added[i], 16)
                    for i in range(TABLES):
                        pool.wait_ge(added[i], 16 * (k + 1))
                n = group_count(pool, mem)
                with pool.Fori(0, n) as g:
                    for h in range(2):
                        pool.wait_ge(rows_made, 2 * g + h + 3)
                        pool.wait_ge(tile_copied, 2 * g + h + 2)
                        pool.sem_inc(mem.turn, 1)
                        for i in range(HALF):
                            u = HALF * h + i
                            pool.wait_ge(added[i], 16 * (2 * g + h) + 48)
                            pool.sem_inc(mem.turn, 1)
                            pool.indirect_dma_start(
                                mem.partial[i], bass.IndirectOffsetOnAxis(ap=rows[:, u:u + 1], axis=0),
                                tile[:, u, :], None, compute_op=ALU.add).then_inc(added[i], 16)
                for i in range(TABLES):
                    pool.wait_ge(added[i], 16 * (2 * n) + 48)


BANK = 512
BATCH = 2
BATCHES = STEPS // BATCH


def steps_of(q):
    return range(BATCH * q, BATCH * q + BATCH)


def copy_indices(nc, mem, index, q, tiles):
    for u in steps_of(q):
        last = nc.scalar.activation(index[:, u:u + 1], mem.src_i[:, bass.ds(tiles[u], 1)], ACT.Copy)
    return last


def build_onehots(nc, mem, into, q, w, t):
    for u in steps_of(q):
        last = nc.vector.tensor_scalar(into[:, u, :], mem.column[:], mem.window_base[:, bass.ds(w[u], 1)],
                                       mem.dst_f[:, bass.ds(t[u], 1)], ALU.add, ALU.is_equal)
    return last


def phase_sum(nc, mem, name, table, features, zero, count):
    with ExitStack() as ctx:
        def sb(tag, shape, dtype=F32):
            return ctx.enter_context(nc.sbuf_tensor(f"{name}_{tag}", shape, dtype))

        width = features + 2
        pitch = BANK if BATCH * width > BANK else width
        index = sb("index", [P, STEPS], I32)
        rows = sb("rows", [P, STEPS, width])
        into = sb("into", [P, STEPS, P])
        sums_ps = [ctx.enter_context(nc.psum_tensor(f"{name}_sums_ps{q}", [P, BATCH, pitch], F32))
                   for q in range(BATCHES)]
        index_in, onehots, summed, added = sems(
            nc, ctx, *(f"{name}_{s}" for s in ("index_in", "onehots", "summed", "added")))
        rows_in = sems(nc, ctx, *(f"{name}_rows_in{q}" for q in range(BATCHES)))
        with nc.Block() as block:
            @block.gpsimd
            def _(pool):
                n, first = count(pool, mem)
                with pool.Fori(0, n) as g:
                    for q in range(BATCHES):
                        pool.wait_ge(index_in, BATCHES * g + q + 1)
                        pool.wait_ge(summed, BATCHES * g + q + 1)
                        pool.sem_inc(mem.turn, 1)
                        for u in steps_of(q):
                            pool.indirect_dma_start(rows[:, u, :], None, table,
                                                    bass.IndirectOffsetOnAxis(ap=index[:, u:u + 1], axis=0)
                                                    ).then_inc(rows_in[q], 16)

            @block.scalar
            def _(act):
                n, first = count(act, mem)
                (t,) = step_registers(act, mem, f"{name}_first", first, tiles=True)
                for q in range(BATCHES):
                    copy_indices(nc, mem, index, q, t).then_inc(index_in, 1)
                with act.Fori(0, n) as g:
                    (t,) = step_registers(act, mem, f"{name}_act", g + first + 1, tiles=True)
                    for q in range(BATCHES):
                        act.wait_ge(rows_in[q], 16 * BATCH * (g + 1))
                        copy_indices(nc, mem, index, q, t).then_inc(index_in, 1)

            @block.vector
            def _(dve):
                if zero:
                    nc.vector.memset(mem.acc[:, :, 0:width], 0.0)
                for q in range(BATCHES):
                    last = nc.vector.memset(sums_ps[q][:], 0.0)
                last.then_inc(added, 1)

                def add_sums(j, q, windows):
                    dve.wait_ge(summed, j + BATCHES - 1)
                    for i, u in enumerate(steps_of(q)):
                        dve.wait_ge(added, BATCH * j + i + 1)
                        acc = window(mem.acc[:, :, 0:width], windows[u])
                        nc.vector.tensor_tensor(acc, acc, sums_ps[q][:, i, 0:width], ALU.add).then_inc(added, 1)

                n, first = count(dve, mem)
                with dve.Fori(0, n) as g:
                    w, t, w_before = step_registers(dve, mem, f"{name}_dve", g + first, windows=True, tiles=True, before=True)
                    for q in range(BATCHES):
                        dve.wait_ge(summed, BATCHES * g + q + 1)
                        build_onehots(nc, mem, into, q, w, t).then_inc(onehots, 1)
                        add_sums(BATCHES * g + q, (q - 2) % BATCHES, w if q >= 2 else w_before)
                (w_before,) = step_registers(dve, mem, f"{name}_dve_last", n + first, before=True)
                for q in range(2):
                    add_sums(BATCHES * n + q, q + 2, w_before)

            @block.tensor
            def _(pe):
                pe.sem_inc(summed, BATCHES)
                n, first = count(pe, mem)
                with pe.Fori(0, n) as g:
                    for q in range(BATCHES):
                        pe.wait_ge(onehots, BATCHES * g + q + 1)
                        pe.wait_ge(rows_in[q], 16 * BATCH * (g + 1))
                        pe.wait_ge(added, BATCH * (BATCHES * g + q) + 1)
                        for i, u in enumerate(steps_of(q)):
                            last = nc.tensor.matmul(sums_ps[q][:, i, 0:width], into[:, u, :], rows[:, u, :],
                                                    start=True, stop=True)
                        last.then_inc(summed, 1)


def phase_weigh(nc, mem):
    with ExitStack() as ctx:
        minus_v = ctx.enter_context(nc.sbuf_tensor("weigh_minus_v", [P, WINDOWS], F32))
        logits = ctx.enter_context(nc.sbuf_tensor("weigh_logits", [P, WINDOWS, 2], F32))
        taken = ctx.enter_context(nc.sbuf_tensor("weigh_taken", [P, WINDOWS, 2], F32))
        chain, weights_made, homo_made, hete_made, stored = sems(
            nc, ctx, "weigh_chain", "weigh_weights_made", "weigh_homo_made", "weigh_hete_made", "weigh_stored")
        chunks = [slice(c, c + CHUNK) for c in range(0, WINDOWS, CHUNK)]
        weights = mem.nodes[:, 0:WINDOWS, 2 * D:2 * D + 2]
        with nc.Block() as block:
            @block.vector
            def _(dve):
                nc.vector.tensor_scalar(minus_v[:], mem.v[:], -1.0, None, ALU.mult).then_inc(chain, 1)
                nc.vector.scalar_tensor_tensor(logits[:, :, 0], mem.v[:], SLOPE, mem.v[:], ALU.mult, ALU.max)
                dve.wait_ge(chain, 1)
                nc.vector.scalar_tensor_tensor(logits[:, :, 1], minus_v[:], SLOPE, minus_v[:],
                                               ALU.mult, ALU.max).then_inc(chain, 1)
                dve.wait_ge(chain, 2)
                nc.vector.tensor_tensor(logits[:], logits[:], mem.shift[:], ALU.subtract).then_inc(chain, 1)
                dve.wait_ge(weights_made, 1)
                nc.vector.scalar_tensor_tensor(taken[:, :, 0], mem.v[:], 0.0, weights[:, :, 0], ALU.is_gt, ALU.mult)
                nc.vector.scalar_tensor_tensor(taken[:, :, 1], mem.v[:], 0.0, weights[:, :, 1],
                                               ALU.is_le, ALU.mult).then_inc(chain, 1)
                dve.wait_ge(chain, 4)
                shape = [P, CHUNK, D]
                for c in chunks:
                    nc.vector.tensor_tensor(mem.nodes[:, c, 0:D], mem.x[:, c, :],
                                            taken[:, c, 0].unsqueeze(2).broadcast_to(shape), ALU.mult)
                    nc.vector.tensor_tensor(mem.nodes[:, c, D:2 * D], mem.x[:, c, :],
                                            taken[:, c, 1].unsqueeze(2).broadcast_to(shape),
                                            ALU.mult).then_inc(homo_made, 1)

            @block.scalar
            def _(act):
                act.wait_ge(chain, 3)
                nc.scalar.activation(weights, logits[:], ACT.Exp).then_inc(weights_made, 1)

            @block.sync
            def _(sp):
                sp.wait_ge(weights_made, 1)
                for n, c in enumerate(chunks):
                    sp.wait_ge(homo_made, n + 1)
                    sp.dma_start(by_window(mem.weighted_rows[c.start * P:c.stop * P, :]),
                                 mem.nodes[:, c, :]).then_inc(stored, 16)
                sp.wait_ge(stored, 16 * len(chunks))


def phase_maxima(nc, mem, v_rows, count):
    with ExitStack() as ctx:
        def sb(name, shape, dtype=F32):
            return ctx.enter_context(nc.sbuf_tensor("max_" + name, shape, dtype))

        index = sb("index", [P, STEPS], I32)
        v = sb("v", [P, STEPS])
        into = sb("into", [P, STEPS, P])
        outside = sb("outside", [P, STEPS, P])
        only = sb("only", [P, STEPS, 2, P])
        best = sb("best", [P, STEPS, 2])
        top = sb("top", [P, WINDOWS, 2])
        only_ps = [ctx.enter_context(nc.psum_tensor(f"max_only_ps{k}", [P, 2, P], F32)) for k in range(STEPS)]
        index_in, chain, only_made, turned, kept = sems(
            nc, ctx, *("max_" + n for n in ("index_in", "chain", "only_made", "turned", "kept")))
        v_in = sems(nc, ctx, "max_v_in")[0]
        with nc.Block() as block:
            @block.gpsimd
            def _(pool):
                n, first = count(pool, mem)
                with pool.Fori(0, n) as g:
                    pool.wait_ge(index_in, g + 1)
                    pool.sem_inc(mem.turn, 1)
                    for u in range(STEPS):
                        pool.indirect_dma_start(v[:, u:u + 1], None, v_rows,
                                                bass.IndirectOffsetOnAxis(ap=index[:, u:u + 1], axis=0)
                                                ).then_inc(v_in, 16)

            @block.scalar
            def _(act):
                act.sem_inc(kept, 1)
                n, first = count(act, mem)
                with act.Fori(0, n) as g:
                    (t,) = step_registers(act, mem, "max_act", g + first, tiles=True)
                    act.wait_ge(kept, STEPS * g + 1)
                    for u in range(STEPS):
                        last = nc.scalar.activation(index[:, u:u + 1], mem.src_i[:, bass.ds(t[u], 1)], ACT.Copy)
                    last.then_inc(index_in, 1)

            @block.vector
            def _(dve):
                nc.vector.memset(top[:], LOWEST).then_inc(chain, 1)
                n, first = count(dve, mem)
                with dve.Fori(0, n) as g:
                    w, t = step_registers(dve, mem, "max_dve", g + first, windows=True, tiles=True)
                    for u in range(STEPS):
                        last = nc.vector.tensor_scalar(into[:, u, :], mem.column[:], mem.window_base[:, bass.ds(w[u], 1)],
                                                       mem.dst_f[:, bass.ds(t[u], 1)], ALU.add, ALU.is_equal)
                    last.then_inc(chain, 1)
                    dve.wait_ge(chain, 3 * g + 2)
                    nc.vector.tensor_scalar(outside[:], into[:], 0.0, LOWEST, ALU.is_equal, ALU.mult).then_inc(chain, 1)
                    dve.wait_ge(chain, 3 * g + 3)
                    dve.wait_ge(v_in, 16 * STEPS * (g + 1))
                    for u in range(STEPS):
                        nc.vector.scalar_tensor_tensor(only[:, u, 0, :], into[:, u, :], v[:, u:u + 1], outside[:, u, :],
                                                       ALU.mult, ALU.add)
                        last = nc.vector.scalar_tensor_tensor(only[:, u, 1, :], into[:, u, :], v[:, u:u + 1],
                                                              outside[:, u, :], ALU.mult, ALU.subtract)
                    last.then_inc(only_made, 1)
                    dve.wait_ge(turned, g + 1)
                    for u in range(STEPS):
                        nc.vector.tensor_reduce(best[:, u, 0:1], only_ps[u][:, 0, :], AX.X, ALU.max)
                        last = nc.vector.tensor_reduce(best[:, u, 1:2], only_ps[u][:, 1, :], AX.X, ALU.min)
                    last.then_inc(chain, 1)
                    dve.wait_ge(chain, 3 * g + 4)
                    for u in range(STEPS):
                        dve.wait_ge(kept, STEPS * g + u + 1)
                        nc.vector.tensor_scalar(window(top, w[u])[:, 0:1], window(top, w[u])[:, 0:1],
                                                best[:, u, 0:1], None, ALU.max)
                        nc.vector.tensor_scalar(window(top, w[u])[:, 1:2], best[:, u, 1:2], -1.0,
                                                window(top, w[u])[:, 1:2], ALU.mult, ALU.max).then_inc(kept, 1)
                dve.wait_ge(kept, STEPS * n + 1)
                dve.wait_ge(chain, 3 * n + 1)
                nc.vector.scalar_tensor_tensor(mem.shift[:], top[:], SLOPE, top[:], ALU.mult, ALU.max)

            @block.tensor
            def _(pe):
                n, first = count(pe, mem)
                with pe.Fori(0, n) as g:
                    pe.wait_ge(only_made, g + 1)
                    for u in range(STEPS):
                        for k in range(2):
                            last = nc.tensor.transpose(only_ps[u][:, k, :], only[:, u, k, :], mem.ident[:])
                    last.then_inc(turned, 1)


def phase_attend(nc, mem, v_rows, count):
    with ExitStack() as ctx:
        def sb(name, shape, dtype=F32):
            return ctx.enter_context(nc.sbuf_tensor("s1_" + name, shape, dtype))

        def ps(name, shape):
            return ctx.enter_context(nc.psum_tensor("s1_" + name, shape, F32))

        index = sb("index", [P, STEPS], I32)
        rows = sb("rows", [P, STEPS, D + 2])
        v = sb("v", [P, STEPS])
        into = sb("into", [P, STEPS, P])
        into_t = sb("into_t", [P, STEPS, P])
        minus_v = sb("minus_v", [P, STEPS])
        logits = sb("logits", [P, STEPS, 2])
        weight = sb("weight", [P, STEPS, 2])
        taken = sb("taken", [P, STEPS, 2])
        weighted = sb("weighted", [P, STEPS, 2 * D])
        into_t_ps = [ps(f"into_t_ps{h}", [P, HALF, P]) for h in range(2)]
        shift_ps = [into_t_ps[h][:, :, 0:2] for h in range(2)]
        sums_ps = [ps(f"sums_ps{k}", [P, 2, 2 * D]) for k in range(HALF)]
        weights_ps = ps("weights_ps", [P, STEPS, 2])
        (index_in, onehots, turned, turned_copied, shifts, chain, exp_in, weights_made, messages, summed,
         added) = sems(nc, ctx, *("s1_" + n for n in (
             "index_in", "onehots", "turned", "turned_copied", "shifts", "chain", "exp_in", "weights_made",
             "messages", "summed", "added")))
        rows_in = sems(nc, ctx, "s1_rows_in")[0]
        with nc.Block() as block:
            @block.gpsimd
            def _(pool):
                n, first = count(pool, mem)
                with pool.Fori(0, n) as g:
                    pool.wait_ge(index_in, g + 1)
                    pool.sem_inc(mem.turn, 1)
                    for u in range(STEPS):
                        place = bass.IndirectOffsetOnAxis(ap=index[:, u:u + 1], axis=0)
                        pool.indirect_dma_start(rows[:, u, :], None, mem.x_rows, place).then_inc(rows_in, 16)
                        pool.indirect_dma_start(v[:, u:u + 1], None, v_rows, place).then_inc(rows_in, 16)

            @block.scalar
            def _(act):
                act.sem_inc(summed, 1)
                n, first = count(act, mem)
                with act.Fori(0, n) as g:
                    (t,) = step_registers(act, mem, "s1_act", g + first, tiles=True)
                    act.wait_ge(summed, g + 1)
                    for u in range(STEPS):
                        last = nc.scalar.activation(index[:, u:u + 1], mem.src_i[:, bass.ds(t[u], 1)], ACT.Copy)
                    last.then_inc(index_in, 1)
                    act.wait_ge(turned, g + 1)
                    for h in range(2):
                        last = nc.scalar.activation(into_t[:, HALF * h:HALF * h + HALF, :], into_t_ps[h][:], ACT.Copy)
                    last.then_inc(turned_copied, 1)
                    act.wait_ge(exp_in, g + 1)
                    nc.scalar.activation(weight[:], logits[:], ACT.Exp).then_inc(weights_made, 1)

            @block.vector
            def _(dve):
                nc.vector.memset(mem.acc[:], 0.0).then_inc(added, 1)
                n, first = count(dve, mem)
                with dve.Fori(0, n) as g:
                    w, t = step_registers(dve, mem, "s1_dve", g + first, windows=True, tiles=True)
                    dve.wait_ge(summed, g + 1)
                    for u in range(STEPS):
                        last = nc.vector.tensor_scalar(into[:, u, :], mem.column[:], mem.window_base[:, bass.ds(w[u], 1)],
                                                       mem.dst_f[:, bass.ds(t[u], 1)], ALU.add, ALU.is_equal)
                    last.then_inc(onehots, 1)
                    dve.wait_ge(rows_in, 32 * STEPS * (g + 1))
                    nc.vector.tensor_scalar(minus_v[:], v[:], -1.0, None, ALU.mult).then_inc(chain, 1)
                    dve.wait_ge(chain, 4 * g + 1)
                    nc.vector.scalar_tensor_tensor(logits[:, :, 0], v[:], SLOPE, v[:], ALU.mult, ALU.max)
                    nc.vector.scalar_tensor_tensor(logits[:, :, 1], minus_v[:], SLOPE, minus_v[:],
                                                   ALU.mult, ALU.max).then_inc(chain, 1)
                    dve.wait_ge(chain, 4 * g + 2)
                    dve.wait_ge(shifts, g + 1)
                    for h in range(2):
                        b = slice(HALF * h, HALF * h + HALF)
                        last = nc.vector.tensor_tensor(logits[:, b, :], logits[:, b, :], shift_ps[h], ALU.subtract)
                    last.then_inc(chain, 1)
                    dve.wait_ge(chain, 4 * g + 3)
                    nc.vector.tensor_scalar(logits[:], logits[:], 0.0, None, ALU.min).then_inc(exp_in, 1)
                    dve.wait_ge(weights_made, g + 1)
                    nc.vector.scalar_tensor_tensor(taken[:, :, 0], v[:], 0.0, weight[:, :, 0], ALU.is_gt, ALU.mult)
                    nc.vector.scalar_tensor_tensor(taken[:, :, 1], v[:], 0.0, weight[:, :, 1],
                                                   ALU.is_le, ALU.mult).then_inc(chain, 1)
                    dve.wait_ge(chain, 4 * g + 4)
                    for u in range(STEPS):
                        for k in range(2):
                            last = nc.vector.tensor_scalar(weighted[:, u, k * D:k * D + D], rows[:, u, 0:D],
                                                           taken[:, u, k:k + 1], None, ALU.mult)
                    last.then_inc(messages, 1)
                    dve.wait_ge(summed, g + 2)
                    for u in range(STEPS):
                        dve.wait_ge(added, STEPS * g + u + 1)
                        acc = window(mem.acc[:, :, 0:2 * D], w[u])
                        small = window(mem.acc[:, :, 2 * D:2 * D + 2], w[u])
                        nc.vector.tensor_tensor(acc, acc, sums_ps[u // 2][:, u % 2, :], ALU.add)
                        nc.vector.tensor_tensor(small, small, weights_ps[:, u, :], ALU.add).then_inc(added, 1)

            @block.tensor
            def _(pe):
                n, first = count(pe, mem)
                with pe.Fori(0, n) as g:
                    (w,) = step_registers(pe, mem, "s1_pe", g + first, windows=True)
                    pe.wait_ge(onehots, g + 1)
                    for u in range(STEPS):
                        last = nc.tensor.transpose(into_t_ps[u // HALF][:, u % HALF, :], into[:, u, :], mem.ident[:])
                    last.then_inc(turned, 1)
                    pe.wait_ge(turned_copied, g + 1)
                    for u in range(STEPS):
                        last = nc.tensor.matmul(shift_ps[u // HALF][:, u % HALF, :], into_t[:, u, :],
                                                window(mem.shift, w[u]), start=True, stop=True)
                    last.then_inc(shifts, 1)
                    pe.wait_ge(messages, g + 1)
                    pe.wait_ge(added, STEPS * g + 1)
                    for u in range(STEPS):
                        nc.tensor.matmul(sums_ps[u // 2][:, u % 2, :], into[:, u, :], weighted[:, u, :],
                                         start=True, stop=True)
                        last = nc.tensor.matmul(weights_ps[:, u, :], into[:, u, :], weight[:, u, :],
                                                start=True, stop=True)
                    last.then_inc(summed, 1)


def phase_gate(nc, mem, edge_attr):
    with ExitStack() as ctx:
        def sb(name, shape, dtype=F32):
            return ctx.enter_context(nc.sbuf_tensor("s3_" + name, shape, dtype))

        def pair(name, shape):
            return [ctx.enter_context(nc.psum_tensor(f"s3_{name}{k}", shape, F32)) for k in range(2)]

        index = sb("index", [P, STEPS], I32)
        rows = sb("rows", [P, STEPS, 2 * D])
        into = sb("into", [P, STEPS, P])
        into_t = sb("into_t", [P, STEPS, P])
        edge = sb("edge", [P, STEPS, P])
        z = sb("z", [P, STEPS, 2 * D])
        soft = mem.acc[:, 0:2 * STEPS, D:2 * D].rearrange("p (s k) d -> p s k d", k=2)
        into_t_ps, z_ps, sums_ps = (pair("into_t_ps", [P, BATCH, P]), pair("z_ps", [P, BATCH, BANK]),
                                    pair("sums_ps", [P, BATCH, D]))
        (cleared, index_in, onehots, turned, turned_copied, products, z_made, abs_made, exp_made, log_made,
         soft_made, gate_made, messages, summed, added) = sems(
            nc, ctx, *("s3_" + n for n in (
                "cleared", "index_in", "onehots", "turned", "turned_copied", "products", "z_made", "abs_made",
                "exp_made", "log_made", "soft_made", "gate_made", "messages", "summed", "added")))
        rows_in = sems(nc, ctx, *(f"s3_rows_in{q}" for q in range(BATCHES)))
        edge_in = sems(nc, ctx, *(f"s3_edge_in{q}" for q in range(BATCHES)))
        Z_CREDIT, PRODUCT_CREDIT = 3, 4

        def span(q):
            q %= BATCHES
            return slice(BATCH * q, BATCH * q + BATCH)

        def halves(ap):
            return ap.rearrange("p s (k d) -> p s k d", k=2)

        with nc.Block() as block:
            @block.gpsimd
            def _(pool):
                n = group_count(pool, mem)
                pool.wait_ge(cleared, 1)
                with pool.Fori(0, n + 1) as g:
                    for q in range(BATCHES):
                        j = BATCHES * g + q
                        pool.wait_ge(index_in, j + 1)
                        pool.wait_ge(z_made, j + 1)
                        pool.sem_inc(mem.turn, 1)
                        for u in steps_of(q):
                            pool.indirect_dma_start(rows[:, u, :], None, mem.b_rows,
                                                    bass.IndirectOffsetOnAxis(ap=index[:, u:u + 1], axis=0)
                                                    ).then_inc(rows_in[q], 16)

            @block.sync
            def _(sp):
                n = group_count(sp, mem)
                with sp.Fori(0, n + 1) as g:
                    (t,) = step_registers(sp, mem, "s3_sp", g, tiles=True)
                    for q in range(BATCHES):
                        sp.wait_ge(products, BATCHES * g + q + 1)
                        for u in steps_of(q):
                            sp.dma_start(edge[:, u, :], edge_attr[:, bass.ds(t[u] * P, P)]).then_inc(edge_in[q], 16)

            @block.scalar
            def _(act):
                (t,) = step_registers(act, mem, "s3_first", 0, tiles=True)
                for q in range(BATCHES):
                    copy_indices(nc, mem, index, q, t).then_inc(index_in, 1)
                act.sem_inc(log_made, 1)
                act.sem_inc(gate_made, 1)
                n = group_count(act, mem)
                act.add_instruction(mybir.InstLoadActFuncSet(name=nc.get_next_instruction_name(),
                                                             act_func_set_id=EXP_LN_SET, engine=act.engine))
                with act.Fori(0, n + 1) as g:
                    (t,) = step_registers(act, mem, "s3_act", g + 1, tiles=True)
                    for q in range(BATCHES):
                        j = BATCHES * g + q
                        last, gate = soft[:, span(q - 1), :, :], soft[:, span(q - 2), 0, :]
                        act.wait_ge(turned, j + 1)
                        nc.scalar.activation(into_t[:, span(q), :], into_t_ps[q % 2][:],
                                             ACT.Copy).then_inc(turned_copied, 1)
                        act.wait_ge(rows_in[q], 16 * BATCH * (g + 1))
                        copy_indices(nc, mem, index, q, t).then_inc(index_in, 1)
                        act.wait_ge(z_made, j + 1 + Z_CREDIT)
                        nc.scalar.activation(last, halves(z[:, span(q - 1), :]), ACT.Abs).then_inc(abs_made, 1)
                        act.wait_ge(soft_made, j + 1)
                        nc.scalar.activation(gate, gate, ACT.Exp, scale=-1.0).then_inc(gate_made, 1)
                        act.wait_ge(abs_made, j + 1)
                        nc.scalar.activation(last, last, ACT.Exp, scale=-1.0).then_inc(exp_made, 1)
                        act.wait_ge(exp_made, j + 1)
                        nc.scalar.activation(last, last, ACT.Ln, bias=1.0).then_inc(log_made, 1)

            @block.vector
            def _(dve):
                for buffer in (rows, into, z, sums_ps[0], sums_ps[1], z_ps[0], z_ps[1], soft, mem.acc[:, :, 0:D]):
                    last = nc.vector.memset(buffer if isinstance(buffer, bass.AP) else buffer[:], 0.0)
                last.then_inc(cleared, 1)
                dve.wait_ge(cleared, 1)
                dve.sem_inc(added, 1)
                dve.sem_inc(z_made, Z_CREDIT)
                n = group_count(dve, mem)
                with dve.Fori(0, n + 1) as g:
                    w, t, w_before = step_registers(dve, mem, "s3_dve", g, windows=True, tiles=True, before=True)

                    def add_sums(q, i):
                        acc = window(mem.acc[:, :, 0:D], w_before[BATCH * q + i])
                        nc.vector.tensor_tensor(acc, acc, sums_ps[q % 2][:, i, :], ALU.add).then_inc(added, 1)

                    for q in range(BATCHES):
                        j = BATCHES * g + q
                        dve.wait_ge(summed, j + 1)
                        build_onehots(nc, mem, into, q, w, t).then_inc(onehots, 1)
                        dve.wait_ge(added, BATCH * j + 1)
                        add_sums(q, 0)
                        dve.wait_ge(gate_made, j + 1)
                        gate, core = soft[:, span(q - 3), 0, :], soft[:, span(q - 3), 1, :]
                        nc.vector.tensor_tensor(core, core, gate, ALU.mult).then_inc(messages, 1)
                        dve.wait_ge(products, j + PRODUCT_CREDIT)
                        dve.wait_ge(index_in, j + BATCHES)
                        nc.vector.tensor_tensor(z[:, span(q - 1), :], rows[:, span(q - 1), :],
                                                z_ps[(q - 1) % 2][:, :, 0:2 * D], ALU.add).then_inc(z_made, 1)
                        dve.wait_ge(added, BATCH * j + 2)
                        add_sums(q, 1)
                        dve.wait_ge(log_made, j + 1)
                        older = soft[:, span(q - 2), :, :]
                        nc.vector.scalar_tensor_tensor(older, halves(z[:, span(q - 2), :]), 0.0, older,
                                                       ALU.max, ALU.add).then_inc(soft_made, 1)

            @block.tensor
            def _(pe):
                pe.sem_inc(products, PRODUCT_CREDIT)
                pe.sem_inc(summed, 1)
                n = group_count(pe, mem)
                with pe.Fori(0, n + 1) as g:
                    (w,) = step_registers(pe, mem, "s3_pe", g, windows=True)
                    for q in range(BATCHES):
                        j = BATCHES * g + q
                        pe.wait_ge(edge_in[q], 16 * BATCH * (g + 1))
                        pe.wait_ge(z_made, j + Z_CREDIT)
                        for i, u in enumerate(steps_of(q)):
                            nc.tensor.matmul(z_ps[q % 2][:, i, 0:2 * D], edge[:, u, :], mem.w3[:, 2, :], start=True, stop=False)
                        pe.wait_ge(onehots, j + 1)
                        for i, u in enumerate(steps_of(q)):
                            last = nc.tensor.transpose(into_t_ps[q % 2][:, i, :], into[:, u, :], mem.ident[:])
                        last.then_inc(turned, 1)
                        pe.wait_ge(messages, j + 1)
                        pe.wait_ge(added, BATCH * j + 1)
                        for i in range(BATCH):
                            u = BATCH * ((q - 3) % BATCHES) + i
                            last = nc.tensor.matmul(sums_ps[(q + 1) % 2][:, i, :], into[:, u, :], soft[:, u, 1, :],
                                                    start=True, stop=True)
                        last.then_inc(summed, 1)
                        pe.wait_ge(turned_copied, j + 1)
                        for i, u in enumerate(steps_of(q)):
                            last = nc.tensor.matmul(z_ps[q % 2][:, i, 0:2 * D], into_t[:, u, :],
                                                    window(mem.nodes[:, :, 0:2 * D], w[u]), start=False, stop=True)
                        last.then_inc(products, 1)


def layer0(nc, mem, a):
    def scale_bias(dve):
        nc.vector.tensor_scalar(mem.b0[:], mem.b0[:], mem.agg[:], None, ALU.mult).then_inc(scaled, 1)
        dve.wait_ge(scaled, 1)

    def message(dve, w, sums):
        return nc.vector.scalar_tensor_tensor(mem.nodes[:, bass.ds(w, 1), 0:D].rearrange("p a b -> p (a b)"), sums[:],
                                              mem.agg[:], mem.b0[:], ALU.mult, ALU.add)

    with nc.semaphore("bias_scaled") as scaled:
        phase_project(nc, mem, "p0", [mem.x], [(0, mem.w0[:])], D, message, scale_bias)
    phase_scatter(nc, mem, a["src_rows"])

    places = [mem.acc[:, :, 0:D], mem.acc[:, :, D:2 * D],
              mem.nodes[:, 0:WINDOWS, 0:D], mem.nodes[:, 0:WINDOWS, D:2 * D]]
    with nc.semaphore("partials_in") as arrived, nc.Block() as block:
        @block.sync
        def _(sp):
            for place, table in zip(places, mem.partial):
                sp.dma_start(place, by_window(table[0:NODES_PAD, :])).then_inc(arrived, 16)
            sp.wait_ge(arrived, 16 * TABLES)

    def add_partials(dve):
        for n, place in enumerate(places):
            nc.vector.tensor_tensor(mem.x, mem.x, place, ALU.add).then_inc(partials_added, 1)
            dve.wait_ge(partials_added, n + 1)

    with nc.semaphore("partials_added") as partials_added:
        phase_norm(nc, mem, "n0", add_partials, (mem.x_rows, True))


def layer1(nc, mem, a):
    phase_weigh(nc, mem)
    phase_maxima(nc, mem, a["node_vec_rows"], groups_if_wide)
    phase_attend(nc, mem, a["node_vec_rows"], groups_if_wide)
    phase_sum(nc, mem, "s1n", mem.weighted_rows, 2 * D, False, groups_unless_wide)
    with ExitStack() as ctx:
        inverse = ctx.enter_context(nc.sbuf_tensor("l1_inverse", [P, WINDOWS, 2], F32))
        (link,) = sems(nc, ctx, "l1_link")
        shape = [P, WINDOWS, D]

        def normalise(dve):
            weights = mem.acc[:, :, 2 * D:2 * D + 2]
            nc.vector.tensor_scalar(weights, weights, 1e-30, None, ALU.max).then_inc(link, 1)
            nc.vector.tensor_tensor(mem.b1[:, 0, :], mem.b1[:, 0, :], mem.b1[:, 1, :], ALU.add).then_inc(link, 1)
            dve.wait_ge(link, 2)
            nc.vector.reciprocal(inverse[:], weights).then_inc(link, 1)
            nc.vector.tensor_tensor(mem.b1[:, 0, :], mem.b1[:, 0, :], mem.b1[:, 2, :], ALU.add).then_inc(link, 1)
            dve.wait_ge(link, 4)
            for j in range(2):
                part = mem.acc[:, :, j * D:j * D + D]
                nc.vector.tensor_tensor(part, part, inverse[:, :, j].unsqueeze(2).broadcast_to(shape),
                                        ALU.mult).then_inc(link, 1)
            dve.wait_ge(link, 6)

        def add_window(dve, w, sums):
            x = window(mem.x, w)
            return nc.vector.tensor_tensor(x, x, sums[:], ALU.add)

        def add_bias(dve):
            nc.vector.tensor_tensor(mem.x, mem.x, mem.b1[:, 0, :].unsqueeze(1).broadcast_to(shape),
                                    ALU.add).then_inc(link, 1)
            dve.wait_ge(link, 7)

        phase_project(nc, mem, "p1", [mem.acc[:, :, 0:D], mem.acc[:, :, D:2 * D], mem.x],
                      [(j, mem.w1[:, j, :]) for j in range(3)], D, add_window, normalise)
        phase_norm(nc, mem, "n1", add_bias, (mem.x_rows, True))


def layer2(nc, mem):
    phase_sum(nc, mem, "s2", mem.x_rows, D, True, all_groups)
    with ExitStack() as ctx:
        def sb(name, shape):
            return ctx.enter_context(nc.sbuf_tensor("l2_" + name, shape, F32))

        inverse = sb("inverse", [P, WINDOWS])
        real = sb("real", [P, WINDOWS])
        square = sb("square", [P, WINDOWS])
        total = sb("total", [P, 2])
        over_all = sb("over_all", [P, 2])
        norm = sb("norm", [P, 2])
        link, tanh_made, squared, total_made, reduced, root_made = sems(
            nc, ctx, *("l2_" + n for n in ("link", "tanh_made", "squared", "total_made", "reduced", "root_made")))
        shape = [P, WINDOWS, D]

        degree = mem.acc[:, :, D]

        def divide(dve):
            nc.vector.tensor_scalar(degree, degree, 1.0, None, ALU.max).then_inc(link, 1)
            dve.wait_ge(link, 1)
            nc.vector.reciprocal(inverse[:], degree).then_inc(link, 1)
            dve.wait_ge(link, 2)
            nc.vector.tensor_tensor(mem.acc[:, :, 0:D], mem.acc[:, :, 0:D],
                                    inverse[:].unsqueeze(2).broadcast_to(shape), ALU.mult).then_inc(link, 1)
            dve.wait_ge(link, 3)

        def with_bias(dve, w, sums):
            return nc.vector.tensor_tensor(window(mem.nodes[:, :, 0:D], w), sums[:], mem.b2[:], ALU.add)

        phase_project(nc, mem, "p2", [mem.x, mem.acc[:, :, 0:D]],
                      [(0, mem.w2[:, 0, :]), (1, mem.w2[:, 1, :]), (0, mem.w2[:, 2, :])], D, with_bias, divide)

        tanhs, squares = mem.nodes[:, 0:WINDOWS, 0:D], mem.acc[:, :, 0:D]
        with nc.Block() as block:
            @block.scalar
            def _(act):
                nc.scalar.activation(tanhs, tanhs, ACT.Tanh).then_inc(tanh_made, 1)
                act.wait_ge(tanh_made, 1)
                nc.scalar.activation(squares, tanhs, ACT.Square).then_inc(squared, 1)
                act.wait_ge(reduced, 1)
                nc.scalar.activation(norm[:], over_all[:], ACT.Sqrt).then_inc(root_made, 1)

            @block.vector
            def _(dve):
                nc.vector.tensor_scalar(real[:], mem.window_base[:], mem.lane[:], float(NODES), ALU.add, ALU.is_lt)
                dve.wait_ge(squared, 1)
                nc.vector.tensor_reduce(square[:], squares, AX.X, ALU.add).then_inc(link, 1)
                dve.wait_ge(link, 4)
                nc.vector.tensor_tensor(square[:], square[:], real[:], ALU.mult).then_inc(link, 1)
                dve.wait_ge(link, 5)
                for k in range(2):
                    last = nc.vector.tensor_reduce(total[:, k:k + 1], square[:], AX.X, ALU.add)
                last.then_inc(total_made, 1)
                dve.wait_ge(root_made, 1)
                nc.vector.reciprocal(total[:], norm[:]).then_inc(link, 1)
                dve.wait_ge(link, 6)

            @block.gpsimd
            def _(pool):
                pool.wait_ge(total_made, 1)
                pool.partition_all_reduce(over_all[:], total[:], P, REDUCE_ADD).then_inc(reduced, 1)

        def add_scaled(dve):
            nc.vector.scalar_tensor_tensor(mem.x, tanhs, total[:, 0:1], mem.x, ALU.mult, ALU.add).then_inc(link, 1)
            dve.wait_ge(link, 7)

        phase_norm(nc, mem, "n2", add_scaled, (mem.x_rows, True))


def layer3(nc, mem, a, out):
    with ExitStack() as ctx:
        link, negated, stored = sems(nc, ctx, "l3_link", "l3_negated", "l3_stored")

        def split(dve, w, sums):
            nc.vector.tensor_tensor(window(mem.nodes[:, :, 0:2 * D], w), sums[:, 0:2 * D], mem.b3[:], ALU.add)
            return nc.vector.tensor_copy(window(mem.acc[:, :, 0:2 * D], w), sums[:, 2 * D:4 * D])

        def negate_gate(dve):
            nc.vector.tensor_scalar(mem.w3[:, :, 0:D], mem.w3[:, :, 0:D], -1.0, None, ALU.mult)
            nc.vector.tensor_scalar(mem.b3[:, 0:D], mem.b3[:, 0:D], -1.0, None, ALU.mult).then_inc(negated, 1)
            dve.wait_ge(negated, 1)

        phase_project(nc, mem, "p3", [mem.x], [(0, mem.w3[:, 0:2, :].rearrange("p a b -> p (a b)"))], 4 * D, split,
                      negate_gate)
        with nc.Block() as block:
            @block.sync
            def _(sp):
                sp.dma_start(by_window(mem.b_rows), mem.acc[:, :, 0:2 * D]).then_inc(stored, 16)
                sp.wait_ge(stored, 16)

        phase_gate(nc, mem, a["edge_attr"])

        def add_acc(dve):
            nc.vector.scalar_tensor_tensor(mem.x, mem.x, 2.0, mem.acc[:, :, 0:D], ALU.mult, ALU.add).then_inc(link, 1)
            dve.wait_ge(link, 1)

        phase_norm(nc, mem, "n3", add_acc, (out, False))




def build(nc, a, out):
    with ExitStack() as ctx:
        mem = Memory(nc, ctx)
        phase_setup(nc, mem, a)
        layer0(nc, mem, a)
        layer1(nc, mem, a)
        layer2(nc, mem)
        layer3(nc, mem, a, out)


def kernel(**inputs):
    import numpy as np
    import concourse.bacc as bacc
    from concourse.bass_utils import run_bass_kernel_spmd

    def edges(name, fill, rows):
        a = np.asarray(inputs[name])
        return np.concatenate([a, np.full(rows * P - EDGES, fill, a.dtype)]).reshape(rows, P)

    def nodes(name):
        a = np.asarray(inputs[name])
        return np.concatenate([a, np.zeros((NODES_PAD - NODES,) + a.shape[1:], a.dtype)])

    def row(name):
        return np.asarray(inputs[name]).reshape(1, -1)

    edge_attr = np.asarray(inputs["edge_attr_128"])
    parts = (3, D, D)
    gate_core = [np.asarray(inputs["L3_gnn_" + n]).reshape(parts) for n in ("W_f", "W_s")]
    arrays = {
        "x": nodes("x"),
        "src_cols": edges("src", 0, TILES_PAD).T,
        "src_rows": edges("src", 0, TILES_PAD),
        "dst_cols": edges("dst", NOWHERE, TILES_PAD).T,
        "dst_tiles": edges("dst", NOWHERE, TILE_ROWS * P).reshape(TILE_ROWS, P, P).transpose(1, 0, 2),
        "edge_attr": np.concatenate([edge_attr, np.zeros((TILES_PAD * P - EDGES, D), edge_attr.dtype)]).T,
        "node_vec_cols": nodes("node_vec").reshape(WINDOWS, P).T,
        "node_vec_rows": nodes("node_vec").reshape(NODES_PAD, 1),
        "L0_W": np.asarray(inputs["L0_gnn_W"]).T,
        "L0_b": row("L0_gnn_b"),
        "L0_gnn_agg_weight": row("L0_gnn_agg_weight"),
        "L1_W_homo": np.asarray(inputs["L1_gnn_W_homo"]),
        "L1_W_hete": np.asarray(inputs["L1_gnn_W_hete"]),
        "L1_W_self": np.asarray(inputs["L1_gnn_W_self"]),
        "L1_b_homo": row("L1_gnn_b_homo"),
        "L1_b_hete": row("L1_gnn_b_hete"),
        "L1_b_self": row("L1_gnn_b_self"),
        "L2_W": np.asarray(inputs["L2_gnn_W"]).T.reshape(3, D, D).transpose(1, 0, 2),
        "L2_b": row("L2_gnn_b"),
        "L3_W": np.stack(gate_core, 2).reshape(3, D, 2 * D).transpose(1, 0, 2),
        "L3_b": np.concatenate([row("L3_gnn_b_f"), row("L3_gnn_b_s")], 1),
    }
    arrays = {n: np.ascontiguousarray(a) for n, a in arrays.items()}
    nc = bacc.Bacc("TRN2", target_bir_lowering=False, num_devices=1)
    a = {n: nc.dram_tensor(n, v.shape, mybir.dt.from_np(v.dtype), kind="ExternalInput").ap()
         for n, v in arrays.items()}
    out = nc.dram_tensor("out", (NODES, D), F32, kind="ExternalOutput").ap()
    build(nc, a, out)
    result = run_bass_kernel_spmd(nc, [arrays], core_ids=[0])
    return result.results[0]["out"]
```
